# Optimizing a Trainium2 kernel written in Bass

```python
import numpy as np
import jax
import jax.numpy as jnp

def _softmax(x, axis=-1):
    return jax.nn.softmax(x, axis=axis)

def _gelu(x):
    return jax.nn.gelu(x, approximate=True)

def _silu(x):
    return jax.nn.silu(x)

def _sigmoid(x):
    return jax.nn.sigmoid(x)

def _layernorm(x, axis=-1, eps=1e-05):
    m = jnp.mean(x, axis=axis, keepdims=True)
    v = jnp.var(x, axis=axis, keepdims=True)
    return (x - m) / jnp.sqrt(v + eps)

def _scatter_add(tgt, idx, src, axis=0):
    return tgt.at[idx].add(src)

def _segment_sum(src, seg, n):
    return jax.ops.segment_sum(src, seg, n)
kernel_name = 'mk_cond_resid_d2_seqx_r2_a6448d'

def setup_inputs(seed: int=0):
    np.random.seed(seed)
    _w = jnp.asarray

    def _rec_inputs():
        import jax
        import jax.numpy as jnp
        _rk = jax.random.key(seed)
        x = -0.000125 + 0.9999 * jax.random.normal(jax.random.fold_in(_rk, 1), (64, 128, 512), jnp.float32)
        _lenS = 128 - jax.random.randint(jax.random.fold_in(_rk, 7), (64,), 0, max(1, 128 // 4) + 1, jnp.int32)
        _lenS2 = 128 - jax.random.randint(jax.random.fold_in(_rk, 8), (64,), 0, max(1, 128 // 4) + 1, jnp.int32)
        cond_1024 = -0.00493535 + 1.00056 * jax.random.normal(jax.random.fold_in(_rk, 11), (64, 512), jnp.float32)
        return (x, cond_1024)
    x, cond_1024 = _rec_inputs()

    def _L0_cond_setup():
        import jax, jax.numpy as jnp
        import numpy as np
        import math
        D = 512
        H = 512
        key = jax.random.key(seed)
        k1, k2, k3, k4 = jax.random.split(key, 4)
        x = jax.random.normal(k1, (64, 256, D), dtype=jnp.float32)
        h0 = jax.random.normal(k2, (64, H), dtype=jnp.float32)
        Wx = jax.random.normal(k3, (D, 4 * H), dtype=jnp.float32) / math.sqrt(D)
        Wh = jax.random.normal(k4, (H, 4 * H), dtype=jnp.float32) / math.sqrt(H)
        b = jnp.zeros((4 * H,), dtype=jnp.float32)
        return {'x': x, 'h0': h0, 'Wx': Wx, 'Wh': Wh, 'b': b}
    _L0_cond_all = _L0_cond_setup()
    _L0_cond_in = {k: v for k, v in _L0_cond_all.items() if k in ('Wx', 'Wh', 'b')}
    del _L0_cond_all

    def _L1_cond_setup():
        import jax, jax.numpy as jnp
        import numpy as np
        import math
        N, T, D, H = (128, 256, 512, 512)
        key = jax.random.key(seed)
        k1, k2, k3, k4 = jax.random.split(key, 4)
        x = jax.random.normal(k1, (N, T, D), dtype=jnp.float32)
        h0 = jax.random.normal(k2, (N, H), dtype=jnp.float32)
        Wx = jax.random.normal(k3, (D, H), dtype=jnp.float32) / math.sqrt(D)
        Wh = jax.random.normal(k4, (H, H), dtype=jnp.float32) / math.sqrt(H)
        b = jnp.zeros((H,), dtype=jnp.float32)
        return {'x': x, 'h0': h0, 'Wx': Wx, 'Wh': Wh, 'b': b}
    _L1_cond_all = _L1_cond_setup()
    _L1_cond_in = {k: v for k, v in _L1_cond_all.items() if k in ('Wx', 'Wh', 'b')}
    del _L1_cond_all
    return {'x': x, 'cond_1024': cond_1024, 'L0_cond_Wx': _L0_cond_in['Wx'], 'L0_cond_Wh': _L0_cond_in['Wh'], 'L0_cond_b': _L0_cond_in['b'], 'L1_cond_Wx': _L1_cond_in['Wx'], 'L1_cond_Wh': _L1_cond_in['Wh'], 'L1_cond_b': _L1_cond_in['b']}

def reference(x, cond_1024, L0_cond_Wx, L0_cond_Wh, L0_cond_b, L1_cond_Wx, L1_cond_Wh, L1_cond_b):
    import jax
    import jax.numpy as jnp

    def _L0_cond_ref(x, h0, Wx, Wh, b):
        import jax, jax.numpy as jnp
        import numpy as np
        import math
        D = 512
        H = 512
        xz = jnp.einsum('ntd,dk->ntk', x, Wx) + b
        c0 = jnp.zeros_like(h0)

        def step(carry, xz_t):
            prev_h, prev_c = carry
            z = xz_t + prev_h @ Wh
            ai, af, ao, ag = jnp.split(z, 4, axis=1)
            i = jax.nn.sigmoid(ai)
            f = jax.nn.sigmoid(af)
            o = jax.nn.sigmoid(ao)
            g = jnp.tanh(ag)
            next_c = f * prev_c + i * g
            next_h = o * jnp.tanh(next_c)
            return ((next_h, next_c), next_h)
        _, hs = jax.lax.scan(step, (h0, c0), jnp.swapaxes(xz, 0, 1))
        return jnp.swapaxes(hs, 0, 1)

    def _L1_cond_ref(x, h0, Wx, Wh, b):
        import jax, jax.numpy as jnp
        import numpy as np
        import math
        N, T, D, H = (128, 256, 512, 512)
        xw = jnp.einsum('ntd,dh->nth', x, Wx) + b

        def step(h_prev, xw_t):
            h_next = jnp.tanh(xw_t + h_prev @ Wh)
            return (h_next, h_next)
        _, hs = jax.lax.scan(step, h0, jnp.swapaxes(xw, 0, 1))
        return jnp.swapaxes(hs, 0, 1)
    x = x + _L0_cond_ref(x, cond_1024, L0_cond_Wx, L0_cond_Wh, L0_cond_b)
    x = x + _L1_cond_ref(x, cond_1024, L1_cond_Wx, L1_cond_Wh, L1_cond_b)
    return x

_drawn_inputs = setup_inputs


def setup_inputs(seed=0):
    import zlib

    import numpy as np

    out = dict(_drawn_inputs(seed))
    spreads = {'L0_cond_b': (0.0, 0.1), 'L1_cond_b': (0.0, 0.1)}
    factors = {}
    for name, (base, spread) in spreads.items():
        noise = np.random.default_rng([zlib.crc32(name.encode()), seed]).standard_normal(out[name].shape)
        drawn = base * np.exp(spread * noise) if base else spread * noise
        out[name] = jnp.asarray(drawn.astype(out[name].dtype))
    for name, factor in factors.items():
        out[name] = (out[name] * factor).astype(out[name].dtype)
    return out
```

```python
from contextlib import ExitStack

import concourse.bass as bass
import concourse.mybir as mybir
from concourse.alu_op_type import AluOpType as ALU

F32 = mybir.dt.float32
F16 = mybir.dt.float16
U32 = mybir.dt.uint32
ACT = mybir.ActivationFunctionType
AX_X = mybir.AxisListType.X
ABSMAX = bass.bass_isa.ReduceOp.absmax

P = 128
N = 64
T = 128
D = 512
C = D // P
G = 4
BT = 4
NB = T // BT
J = 2
W = C * N
HIDDEN_SCALE = 2.0 ** 14
EXPONENT_MASK = 0x7F800000
SMALLEST_MAX = 2.0 ** -100

GATE_COLUMNS = [g * D + c * P for g in (0, 3, 1, 2) for c in range(C)]
IG_CHUNKS = range(0, 2 * C)
FO_CHUNKS = range(2 * C, 4 * C)
M0 = G * C
CHUNKS_IN_STEP = [range(0, 0), range(0, 5), range(5, 10), range(10, 16)]


class Block:

    def __init__(self, b, parity, half, known=None):
        self.b, self.parity, self.half = b, parity, half
        k = self.known = known if known is not None else 2
        self.lstm = 0 <= k < NB
        self.rnn = 1 <= k <= NB
        self.rnn_before = 2 <= k <= NB + 1
        self.out = 2 <= k <= NB + 1
        self.next_x = k + 1 < NB
        self.load_x = k + 2 < NB
        self.first = k == 0
        self.rnn_first = k == 1
        self.steady = k >= 2
        self.prologue = k == -1

    def evacuated_before(self):
        if self.steady:
            return 2 * M0 + (M0 + C) * (self.b - 1) - (0 if self.known < NB else M0)
        return {-1: 0, 0: M0, 1: 2 * M0}[self.b]

    def rnn_chunk(self, m):
        return self.evacuated_before() + m

    def lstm_chunk(self, m):
        return self.evacuated_before() + (C if self.rnn else 0) + m


def known_block(b):
    return Block(b, b % 2, b // 2, known=b)


def run_blocks(engine, emit):
    for b in (-1, 0, 1):
        emit(known_block(b))
    with engine.Fori(1, NB // 2 - 1) as i:
        emit(Block(2 * i, 0, i))
        emit(Block(2 * i + 1, 1, i))
    for b in (NB - 2, NB - 1, NB, NB + 1):
        emit(known_block(b))


def build(nc, x, h0, Wx0, Wh0, b0, Wx1, Wh1, b1, out):
    with ExitStack() as ctx:
        def sb(name, shape, dt=F32):
            return ctx.enter_context(nc.sbuf_tensor(name, shape, dt))

        def psum(name, shape):
            return ctx.enter_context(nc.psum_tensor(name, shape, F32))

        def sem(name):
            return ctx.enter_context(nc.semaphore(name))

        wx0 = [sb(f"wx0_{part}", [P, C, G * D], F16) for part in ("hi", "lo")]
        wh0 = [sb(f"wh0_{part}", [P, C, G * D], F16) for part in ("hi", "lo")]
        wx1 = [sb(f"wx1_{part}", [P, C, D], F16) for part in ("hi", "lo")]
        wh1 = [sb(f"wh1_{part}", [P, C, D], F16) for part in ("hi", "lo")]

        arena = sb("arena", [P, 2 * C * G * D])
        stage_wx0 = arena[:, 0:C * G * D].rearrange("p (k n) -> p k n", k=C)
        stage_wh0 = arena[:, C * G * D:2 * C * G * D].rearrange("p (k n) -> p k n", k=C)
        stage_wx1 = sb("stage_wx1", [P, C, D])
        stage_wh1 = sb("stage_wh1", [P, C, D])
        used = [0]

        def from_arena(columns):
            used[0] += columns
            return arena[:, used[0] - columns:used[0]]

        xz = [from_arena(M0 * BT * N).rearrange("p (m q) -> p m q", m=M0) for _ in range(2)]
        assert used[0] == C * G * D
        y1 = [from_arena(BT * W).rearrange("p (q c n) -> p q c n", q=BT, c=C) for _ in range(2)]
        y1_parts = [[from_arena(BT * W // 2).bitcast(F16).rearrange("p (c q) -> p c q", c=C)
                     for _ in range(2)] for _ in range(2)]
        rxz = from_arena(C * BT * N).rearrange("p (m q) -> p m q", m=C)
        outT = from_arena(J * D * 1).rearrange("p (j c q) -> p j c q", j=J, c=C)
        out_rows = from_arena(J * D).rearrange("p (j d) -> p j d", j=J)
        assert used[0] <= 2 * C * G * D

        x_rows = [sb(f"x_rows{i}", [P, J, D]) for i in range(2)]
        xT = [sb(f"xT{i}", [P, J, C, P]) for i in range(2)]
        x_parts = [sb(f"x_{part}", [P, J, C, P], F16) for part in ("hi", "lo")]
        h0_rows = sb("h0_rows", [N, D])
        bias_rows = sb("bias_rows", [M0 + C, P])
        bias = sb("bias", [P, M0 + C])
        ident = sb("ident", [P, P])

        z_ig = sb("z_ig", [P, 2 * C, N])
        z_fo = sb("z_fo", [P, 2 * C, N])
        gate_i, gate_g, gate_f, gate_o = (sb(f"gate_{g}", [P, W]) for g in "igfo")
        i_times_g = sb("i_times_g", [P, W])
        f_times_c = sb("f_times_c", [P, W])
        cell = sb("cell", [P, W])
        tanh_cell = sb("tanh_cell", [P, W])
        h_scaled = sb("h_scaled", [P, W])
        h_parts = [sb(f"h_{part}", [P, W], F16) for part in ("hi", "lo")]
        rnn_z = sb("rnn_z", [P, C, N])
        rnn_h = sb("rnn_h", [P, W])
        rnn_parts = [sb(f"rnn_h_{part}", [P, W], F16) for part in ("hi", "lo")]

        x_max_rows = sb("x_max_rows", [P, 1])
        x_max = [sb(f"x_max{i}", [P, 1]) for i in range(2)]
        y_max = sb("y_max", [P, 1])
        inv_x, inv_y = sb("inv_x", [P, 1]), [sb(f"inv_y{i}", [P, 1]) for i in range(2)]
        scale_x, scale_y = sb("scale_x", [P, 1]), [sb(f"scale_y{i}", [P, 1]) for i in range(2)]
        unscale_x = [sb(f"unscale_x{i}", [P, 1]) for i in range(2)]
        unscale_y = sb("unscale_y", [P, 1])
        NAMES = ("wx0", "wh0", "wx1", "wh1", "h0")
        piece_max = {n: sb(f"piece_max_{n}", [P, C]) for n in NAMES}
        part_max = {n: sb(f"part_max_{n}", [P, 1]) for n in NAMES}
        all_max = {n: sb(f"all_max_{n}", [P, 1]) for n in NAMES}
        inv = {n: sb(f"inv_{n}", [P, 1]) for n in NAMES}
        scale = {n: sb(f"scale_{n}", [P, 1]) for n in NAMES}
        unscale_h, unscale_first = sb("unscale_h", [P, 1]), sb("unscale_first", [P, 1])
        rnn_unscale_h, rnn_unscale_first = sb("rnn_unscale_h", [P, 1]), sb("rnn_unscale_first", [P, 1])

        ps_ig = psum("ps_ig", [P, 2 * C, N])
        ps_fo = psum("ps_fo", [P, 2 * C, N])
        ps_rnn = psum("ps_rnn", [P, 512])
        ps_proj = [psum(f"ps_proj{i}", [P, 512]) for i in range(2)]
        ps_turn = [psum(f"ps_turn{i}", [P, 512]) for i in range(2)]

        w_loaded = {n: sem(f"w_loaded_{n}") for n in NAMES[:4]}
        biases_turned, biases_read = sem("biases_turned"), sem("biases_read")
        x_loaded = [sem(f"x_loaded{i}") for i in range(2)]
        moved = sem("moved")
        SMALL = 5 * 16
        ident_zeroed, ident_ready = sem("ident_zeroed"), sem("ident_ready")
        w_pieces_maxed = sem("w_pieces_maxed")
        w_part_maxed = sem("w_part_maxed")
        w_all_maxed = sem("w_all_maxed")
        scale_steps = sem("scale_steps")
        block_steps = sem("block_steps")
        w_scaled = sem("w_scaled")
        w_hi_ready = sem("w_hi_ready")
        w_lo_ready = sem("w_lo_ready")
        h0_turned = sem("h0_turned")
        h0_hi_ready, h0_lo_ready = sem("h0_hi_ready"), sem("h0_lo_ready")
        unscales_ready = sem("unscales_ready")
        x_maxed = sem("x_maxed")
        x_all_maxed = sem("x_all_maxed")
        x_scaled = sem("x_scaled")
        y_unscaled = sem("y_unscaled")
        x_turned = sem("x_turned")
        x_hi_ready = sem("x_hi_ready")
        x_lo_ready = sem("x_lo_ready")
        proj_done, proj_read = sem("proj_done"), sem("proj_read")
        ig_done, fo_done, rnn_done = sem("ig_done"), sem("fo_done"), sem("rnn_done")
        z_ig_ready, z_fo_ready = sem("z_ig_ready"), sem("z_fo_ready")
        ig_ready, f_ready, o_ready = sem("ig_ready"), sem("f_ready"), sem("o_ready")
        products_ready = sem("products_ready")
        cell_ready, tanh_cell_ready = sem("cell_ready"), sem("tanh_cell_ready")
        h_scaled_ready, h_hi_ready, h_ready = sem("h_scaled_ready"), sem("h_hi_ready"), sem("h_ready")
        y_ready, y_hi_ready, y_lo_ready = sem("y_ready"), sem("y_hi_ready"), sem("y_lo_ready")
        rnn_z_ready, rnn_tanh_ready = sem("rnn_z_ready"), sem("rnn_tanh_ready")
        rnn_hi_ready, rnn_ready = sem("rnn_hi_ready"), sem("rnn_ready")
        out_summed = sem("out_summed")
        out_turned = sem("out_turned")
        out_copied = sem("out_copied")

        PIECES = {"wx0": C, "wh0": C, "wx1": 1, "wh1": 1}
        PIECES_TO = {"wx0": C, "wh0": 2 * C, "wx1": 2 * C + 1, "wh1": 2 * C + 2}
        STAGE = {"wx0": stage_wx0, "wh0": stage_wh0, "wx1": stage_wx1, "wh1": stage_wh1}
        PARTS = {"wx0": wx0, "wh0": wh0, "wx1": wx1, "wh1": wh1}
        SOURCE = {"wx0": Wx0, "wh0": Wh0, "wx1": Wx1, "wh1": Wh1}

        def piece(name, tensor, k):
            return tensor[:, k, :] if PIECES[name] == C else tensor[:, :, :]

        def both_halves(engine, dram, b):
            pairs = dram.rearrange("n (b r) d -> n b (r d)", r=BT // 2)
            starts = [2 * b + tb if isinstance(b, int) else engine.snap(2 * b + tb) for tb in range(2)]
            return [pairs[:, bass.ds(start, 1), :].rearrange("n o e -> n (o e)") for start in starts]

        block = ctx.enter_context(nc.Block())

        @block.sync
        def _(sp):
            def load_x(parity, halves):
                for tb, rows in enumerate(halves):
                    sp.dma_start(x_rows[parity][tb * N:(tb + 1) * N, :, :].rearrange("p j d -> p (j d)"),
                                 rows).then_inc(x_loaded[parity], 16)

            def load_weights(name):
                rows = SOURCE[name].rearrange("(k p) n -> p k n", p=P)
                for k in range(C):
                    sp.dma_start(STAGE[name][:, k, :], rows[:, k, :]).then_inc(w_loaded[name], 16)

            load_x(0, both_halves(sp, x, 0))
            load_weights("wx0")
            sp.dma_start(h0_rows[:, :], h0).then_inc(moved, 16)
            load_weights("wh0")
            load_weights("wx1")
            load_weights("wh1")

            def blocks(k):
                loads = both_halves(sp, x, k.b + 2) if k.load_x else []
                stores = both_halves(sp, out, k.b - 2) if k.out else []
                if k.load_x:
                    if not k.prologue:
                        sp.wait_ge(x_maxed, k.b + 1)
                        sp.wait_ge(x_turned, 2 * k.b + 2)
                    load_x(k.parity, loads)
                if k.out:
                    sp.wait_ge(out_copied, 2 * k.b - 2)
                    for tb, rows in enumerate(stores):
                        sp.dma_start(rows, out_rows[tb * N:(tb + 1) * N, :, :].rearrange("p j d -> p (j d)")
                                     ).then_inc(moved, 16)

            run_blocks(sp, blocks)
            sp.wait_ge(moved, SMALL + 32 * NB)

        @block.gpsimd
        def _(pool):
            nc.gpsimd.memset(ident[:, :], 0.0).then_inc(ident_zeroed, 1)
            pool.wait_ge(ident_zeroed, 1)
            nc.gpsimd.affine_select(out=ident[:, :], in_=ident[:, :], compare_op=ALU.not_equal, fill=1.0,
                                    base=0, pattern=[[-1, P]], channel_multiplier=1).then_inc(ident_ready, 1)

            def max_of_x(b, parity):
                count = b + 1 if isinstance(b, int) else pool.to_reg(b + 1)
                pool.wait_ge(ident_ready, 1)
                pool.wait_ge(x_maxed, count)
                nc.gpsimd.partition_all_reduce(x_max[parity][:, :], x_max_rows[:, :], P,
                                               ABSMAX).then_inc(x_all_maxed, 1)

            def max_of_weights(name):
                pool.wait_ge(w_part_maxed, NAMES.index(name) + 1)
                nc.gpsimd.partition_all_reduce(all_max[name][:, :], part_max[name][:, :], P,
                                               ABSMAX).then_inc(w_all_maxed, 1)

            max_of_x(0, 0)
            max_of_weights("wx0")

            def blocks(k):
                if k.load_x:
                    max_of_x(k.b + 2, k.parity)
                if k.prologue:
                    for name in NAMES[1:]:
                        max_of_weights(name)

            run_blocks(pool, blocks)

        @block.scalar
        def _(act):
            gates = b0.rearrange("(m p) -> m p", p=P)
            for to, of, count in ((0, 0, C), (C, 3 * C, C), (2 * C, C, 2 * C)):
                act.dma_start(bias_rows[to:to + count, :], gates[of:of + count, :]).then_inc(moved, 16)
            act.dma_start(bias_rows[M0:M0 + C, :], b1.rearrange("(m p) -> m p", p=P)).then_inc(moved, 16)

            def hi_of_weights(name):
                act.wait_ge(w_scaled, NAMES.index(name) + 1)
                for k in range(PIECES[name]):
                    nc.scalar.activation(piece(name, PARTS[name][0], k), piece(name, STAGE[name], k),
                                         ACT.Copy, scale=scale[name][:, :]).then_inc(w_hi_ready, 1)

            def read_lstm_chunk(k, m):
                act.wait_ge(proj_done, k.lstm_chunk(m) + 1)
                nc.scalar.activation(xz[1 - k.parity][:, m, :], ps_proj[m % 2][:, 0:BT * N], ACT.Identity,
                                     bias=bias[:, m:m + 1],
                                     scale=unscale_x[1 - k.parity][:, :]).then_inc(proj_read, 1)

            def read_rnn_chunk(k, m):
                act.wait_ge(proj_done, k.rnn_chunk(m) + 1)
                nc.scalar.activation(rxz[:, m, :], ps_proj[m % 2][:, 0:BT * N], ACT.Identity,
                                     bias=bias[:, M0 + m:M0 + m + 1],
                                     scale=unscale_y[:, :]).then_inc(proj_read, 1)

            def read_x(k, j):
                act.wait_ge(x_turned, 2 * (k.b + 1) + j + 1)
                turned = ps_turn[j][:, :].rearrange("p (c q) -> p c q", c=C)
                nc.scalar.activation(xT[1 - k.parity][:, j, :, :], turned, ACT.Copy)
                nc.scalar.activation(x_parts[0][:, j, :, :], turned, ACT.Copy,
                                     scale=scale_x[:, :]).then_inc(x_hi_ready, 1)

            hi_of_weights("wx0")
            act.wait_ge(biases_turned, 1)
            nc.scalar.activation(bias[:, :], ps_turn[1][:, 0:M0 + C], ACT.Copy).then_inc(biases_read, 1)

            def blocks(k):
                for s in range(BT):
                    t = BT * k.b + s
                    if s == 0:
                        chunks = [(read_rnn_chunk, m) for m in range(C)] if k.rnn else []
                    else:
                        chunks = [(read_lstm_chunk, m) for m in CHUNKS_IN_STEP[s]] if k.next_x else []

                    def read_chunks(count):
                        for read, m in chunks[:count]:
                            read(k, m)
                        del chunks[:count]

                    if k.rnn_before if s == 0 else k.rnn:
                        act.wait_ge(rnn_z_ready, t - BT)
                        if k.steady or s >= 2:
                            act.wait_ge(out_summed, t - 1 - BT)
                            act.wait_ge(rnn_ready, t - 1 - BT)
                        nc.scalar.activation(rnn_h[:, :], rnn_z[:, :, :].rearrange("p c n -> p (c n)"),
                                             ACT.Tanh).then_inc(rnn_tanh_ready, 1)
                    if s == 0 and k.rnn:
                        act.wait_ge(y_unscaled, k.b)
                        if k.rnn_before:
                            act.wait_ge(rnn_z_ready, BT * (k.b - 1))
                    if k.lstm:
                        act.wait_ge(z_ig_ready, t + 1)
                        nc.scalar.activation(gate_i[:, :].rearrange("p (c n) -> p c n", c=C), z_ig[:, 0:C, :],
                                             ACT.Sigmoid)
                        nc.scalar.activation(gate_g[:, :].rearrange("p (c n) -> p c n", c=C), z_ig[:, C:2 * C, :],
                                             ACT.Tanh).then_inc(ig_ready, 1)
                        act.wait_ge(z_fo_ready, t + 1)
                        nc.scalar.activation(gate_f[:, :].rearrange("p (c n) -> p c n", c=C), z_fo[:, 0:C, :],
                                             ACT.Sigmoid).then_inc(f_ready, 1)
                        nc.scalar.activation(gate_o[:, :].rearrange("p (c n) -> p c n", c=C), z_fo[:, C:2 * C, :],
                                             ACT.Sigmoid).then_inc(o_ready, 1)
                        if s > 0:
                            read_chunks(1)
                        act.wait_ge(cell_ready, t + 1)
                        nc.scalar.activation(tanh_cell[:, :], cell[:, :], ACT.Tanh).then_inc(tanh_cell_ready, 1)
                        read_chunks(1 if s == 0 else 2)
                        j, tb = s % 2, s // 2
                        act.wait_ge(y_ready, t + 1)
                        nc.scalar.activation(
                            y1_parts[k.parity][0][:, :, (2 * j + tb) * N:(2 * j + tb + 1) * N],
                            y1[k.parity][:, 2 * j + tb, :, :], ACT.Copy,
                            scale=scale_y[k.parity][:, :]).then_inc(y_hi_ready, 1)
                    read_chunks(len(chunks))
                    if s == 0 and k.next_x:
                        act.wait_ge(x_scaled, k.b + 2)
                        for j in range(J):
                            read_x(k, j)
                    if k.prologue and s == 2:
                        hi_of_weights("wh0")
                if k.prologue:
                    hi_of_weights("wx1")
                    hi_of_weights("wh1")
                    act.wait_ge(w_scaled, len(NAMES))
                    nc.scalar.activation(h_parts[0][:, :], ps_rnn[:, 0:W], ACT.Copy,
                                         scale=scale["h0"][:, :])
                    nc.scalar.activation(rnn_parts[0][:, :], ps_rnn[:, 0:W], ACT.Copy,
                                         scale=scale["h0"][:, :]).then_inc(h0_hi_ready, 1)

            run_blocks(act, blocks)

        @block.vector
        def _(dve):
            own = [0]

            def scale_step(instruction):
                own[0] += 1
                instruction.then_inc(scale_steps, 1)
                dve.wait_ge(scale_steps, own[0])

            def power_below(result, maximum):
                bits = result.bitcast(U32)
                yield nc.vector.tensor_scalar(result, maximum, SMALLEST_MAX, None, ALU.max)
                yield nc.vector.tensor_scalar(bits, bits, EXPONENT_MASK, None, ALU.bitwise_and)
                yield nc.vector.tensor_scalar(result, result, 1.0 / HIDDEN_SCALE, None, ALU.mult)

            def max_of_weights(name):
                for k in range(PIECES[name]):
                    dve.wait_ge(w_loaded[name], 16 * C)
                    source = piece(name, STAGE[name], k)
                    if PIECES[name] == 1:
                        source = source.rearrange("p k n -> p (k n)")
                    last = nc.vector.tensor_reduce(piece_max[name][:, k:k + 1], source, AX_X, ALU.max,
                                                   apply_absolute_value=True)
                last.then_inc(w_pieces_maxed, 1)
                dve.wait_ge(w_pieces_maxed, NAMES.index(name) + 1)
                nc.vector.tensor_reduce(part_max[name][:, :], piece_max[name][:, 0:PIECES[name]], AX_X,
                                        ALU.max).then_inc(w_part_maxed, 1)

            def scale_of_weights(name):
                dve.wait_ge(w_all_maxed, NAMES.index(name) + 1)
                for step in power_below(inv[name][:, :], all_max[name][:, :]):
                    scale_step(step)
                nc.vector.reciprocal(scale[name][:, :], inv[name][:, :]).then_inc(w_scaled, 1)

            def lo_of_weights(name):
                dve.wait_ge(w_scaled, NAMES.index(name) + 1)
                for k in range(PIECES[name]):
                    dve.wait_ge(w_hi_ready, PIECES_TO[name] - PIECES[name] + k + 1)
                    a, h, l = (piece(name, v, k) for v in (STAGE[name], PARTS[name][0], PARTS[name][1]))
                    nc.vector.scalar_tensor_tensor(l, a, scale[name][:, :], h, ALU.mult,
                                                   ALU.subtract).then_inc(w_lo_ready, 1)

            def max_of_x(b, parity, half):
                dve.wait_ge(x_loaded[parity], 32 * half + 32)
                nc.vector.tensor_reduce(x_max_rows[:, :], x_rows[parity][:, :, :].rearrange("p j d -> p (j d)"),
                                        AX_X, ALU.max, apply_absolute_value=True).then_inc(x_maxed, 1)

            def scales_of_block(b, parity):
                dve.wait_ge(x_all_maxed, b + 1)
                nc.vector.tensor_scalar(y_max[:, :], x_max[parity][:, :], 1.0, None, ALU.add
                                        ).then_inc(block_steps, 1)
                count = 7 * b + 1
                for maximum, result in ((x_max[parity], inv_x), (y_max, inv_y[parity])):
                    for step in power_below(result[:, :], maximum[:, :]):
                        step.then_inc(block_steps, 1)
                        count = count + 1
                        dve.wait_ge(block_steps, count)
                nc.vector.reciprocal(scale_x[:, :], inv_x[:, :])
                nc.vector.reciprocal(scale_y[parity][:, :], inv_y[parity][:, :])
                nc.vector.tensor_tensor(unscale_x[parity][:, :], inv_x[:, :], inv["wx0"][:, :],
                                        ALU.mult).then_inc(x_scaled, 1)

            max_of_x(0, 0, 0)
            max_of_weights("wx0")
            scale_of_weights("wx0")
            lo_of_weights("wx0")

            def lstm_step(k, s):
                t = BT * k.b + s
                j, tb = s % 2, s // 2
                q = 2 * j + tb
                here = slice(q * N, (q + 1) * N)
                unscale = unscale_first if k.first and s == 0 else unscale_h
                dve.wait_ge(ig_done, t + 1)
                nc.vector.scalar_tensor_tensor(z_ig[:, :, :], ps_ig[:, :, :], unscale[:, :],
                                               xz[k.parity][:, 0:2 * C, here], ALU.mult,
                                               ALU.add).then_inc(z_ig_ready, 1)
                dve.wait_ge(ig_ready, t + 1)
                nc.vector.tensor_tensor(i_times_g[:, :], gate_i[:, :], gate_g[:, :],
                                        ALU.mult).then_inc(products_ready, 1)
                dve.wait_ge(fo_done, t + 1)
                nc.vector.scalar_tensor_tensor(z_fo[:, :, :], ps_fo[:, :, :], unscale[:, :],
                                               xz[k.parity][:, 2 * C:4 * C, here], ALU.mult,
                                               ALU.add).then_inc(z_fo_ready, 1)
                dve.wait_ge(f_ready, t + 1)
                nc.vector.tensor_tensor(f_times_c[:, :], gate_f[:, :], cell[:, :],
                                        ALU.mult).then_inc(products_ready, 1)
                dve.wait_ge(products_ready, 2 * t + 2)
                nc.vector.tensor_tensor(cell[:, :], f_times_c[:, :], i_times_g[:, :],
                                        ALU.add).then_inc(cell_ready, 1)
                dve.wait_ge(o_ready, t + 1)
                dve.wait_ge(tanh_cell_ready, t + 1)
                nc.vector.scalar_tensor_tensor(h_scaled[:, :], gate_o[:, :], HIDDEN_SCALE, tanh_cell[:, :],
                                               ALU.mult, ALU.mult).then_inc(h_scaled_ready, 1)
                dve.wait_ge(h_scaled_ready, t + 1)
                nc.vector.tensor_copy(h_parts[0][:, :], h_scaled[:, :]).then_inc(h_hi_ready, 1)
                dve.wait_ge(h_hi_ready, t + 1)
                nc.vector.tensor_tensor(h_parts[1][:, :], h_scaled[:, :], h_parts[0][:, :],
                                        ALU.subtract).then_inc(h_ready, 1)
                nc.vector.scalar_tensor_tensor(
                    y1[k.parity][:, q, :, :], h_scaled[:, :].rearrange("p (c n) -> p c n", c=C),
                    1.0 / HIDDEN_SCALE, xT[k.parity][:, j, :, tb * N:(tb + 1) * N], ALU.mult,
                    ALU.add).then_inc(y_ready, 1)
                dve.wait_ge(y_hi_ready, t + 1)
                nc.vector.scalar_tensor_tensor(
                    y1_parts[k.parity][1][:, :, here], y1[k.parity][:, q, :, :], scale_y[k.parity][:, :],
                    y1_parts[k.parity][0][:, :, here], ALU.mult, ALU.subtract).then_inc(y_lo_ready, 1)

            def rnn_step(k, s):
                r = BT * k.b + s - 1 - BT
                q_step = (s - 1) % BT
                q = 2 * (q_step % 2) + q_step // 2
                unscale = rnn_unscale_first if k.rnn_first and s == 1 else rnn_unscale_h
                if s == 1:
                    dve.wait_ge(proj_read, k.rnn_chunk(C))
                dve.wait_ge(rnn_done, r + 1)
                nc.vector.scalar_tensor_tensor(
                    rnn_z[:, :, :], ps_rnn[:, 0:W].rearrange("p (c n) -> p c n", c=C), unscale[:, :],
                    rxz[:, :, q * N:(q + 1) * N], ALU.mult, ALU.add).then_inc(rnn_z_ready, 1)
                dve.wait_ge(rnn_tanh_ready, r + 1)
                nc.vector.tensor_scalar(rnn_parts[0][:, :], rnn_h[:, :], HIDDEN_SCALE, None,
                                        ALU.mult).then_inc(rnn_hi_ready, 1)
                dve.wait_ge(rnn_hi_ready, r + 1)
                nc.vector.scalar_tensor_tensor(rnn_parts[1][:, :], rnn_h[:, :], HIDDEN_SCALE,
                                               rnn_parts[0][:, :], ALU.mult,
                                               ALU.subtract).then_inc(rnn_ready, 1)
                j, tb = q_step % 2, q_step // 2
                nc.vector.tensor_tensor(
                    outT[:, j, :, tb * N:(tb + 1) * N], y1[k.parity if s == 0 else 1 - k.parity][:, q, :, :],
                    rnn_h[:, :].rearrange("p (c n) -> p c n", c=C), ALU.add).then_inc(out_summed, 1)

            def blocks(k):
                for s in range(BT):
                    if s == 1 and k.next_x:
                        for j in range(J):
                            dve.wait_ge(x_hi_ready, 2 * (k.b + 1) + j + 1)
                            nc.vector.scalar_tensor_tensor(
                                x_parts[1][:, j, :, :].rearrange("p c q -> p (c q)"),
                                xT[1 - k.parity][:, j, :, :].rearrange("p c q -> p (c q)"), scale_x[:, :],
                                x_parts[0][:, j, :, :].rearrange("p c q -> p (c q)"), ALU.mult,
                                ALU.subtract).then_inc(x_lo_ready, 1)
                    if k.rnn_before if s == 0 else k.rnn:
                        rnn_step(k, s)
                    if s == 0 and k.rnn:
                        nc.vector.tensor_tensor(unscale_y[:, :], inv_y[1 - k.parity][:, :], inv["wx1"][:, :],
                                                ALU.mult).then_inc(y_unscaled, 1)
                        dve.wait_ge(y_unscaled, k.b)
                    if k.lstm:
                        lstm_step(k, s)
                    if s == 0 and k.out:
                        for j in range(J):
                            dve.wait_ge(out_turned, 2 * (k.b - 2) + j + 1)
                            if j == 0:
                                dve.wait_ge(moved, SMALL + 32 * (k.b - 2))
                            nc.vector.tensor_copy(out_rows[:, j, :], ps_turn[j][:, :]).then_inc(out_copied, 1)
                    if s == 0 and k.next_x:
                        scales_of_block(k.b + 1, 1 - k.parity)
                    if s == BT - 1 and k.load_x:
                        dve.wait_ge(x_all_maxed, k.b + 2)
                        max_of_x(k.b + 2, k.parity, k.half + 1)
                if k.prologue:
                    nc.vector.memset(cell[:, :], 0.0)
                    max_of_weights("wh0")
                    max_of_weights("wx1")
                    scale_of_weights("wh0")
                    lo_of_weights("wh0")
                    max_of_weights("wh1")
                    dve.wait_ge(h0_turned, 1)
                    nc.vector.tensor_reduce(part_max["h0"][:, :], ps_rnn[:, 0:W], AX_X, ALU.max,
                                            apply_absolute_value=True).then_inc(w_part_maxed, 1)
                    for name in ("wx1", "wh1", "h0"):
                        scale_of_weights(name)
                    dve.wait_ge(w_scaled, len(NAMES))
                    nc.vector.tensor_scalar(unscale_h[:, :], inv["wh0"][:, :], 1.0 / HIDDEN_SCALE, None, ALU.mult)
                    nc.vector.tensor_tensor(unscale_first[:, :], inv["wh0"][:, :], inv["h0"][:, :], ALU.mult)
                    nc.vector.tensor_scalar(rnn_unscale_h[:, :], inv["wh1"][:, :], 1.0 / HIDDEN_SCALE, None,
                                            ALU.mult)
                    nc.vector.tensor_tensor(rnn_unscale_first[:, :], inv["wh1"][:, :], inv["h0"][:, :],
                                            ALU.mult).then_inc(unscales_ready, 1)
                    lo_of_weights("wx1")
                    lo_of_weights("wh1")
                    dve.wait_ge(h0_hi_ready, 1)
                    for parts in (h_parts, rnn_parts):
                        nc.vector.scalar_tensor_tensor(parts[1][:, :], ps_rnn[:, 0:W], scale["h0"][:, :],
                                                       parts[0][:, :], ALU.mult,
                                                       ALU.subtract).then_inc(h0_lo_ready, 1)
                    dve.wait_ge(unscales_ready, 1)

            run_blocks(dve, blocks)

        @block.tensor
        def _(pe):
            def products(result, weights, columns, moving):
                terms = [(k, w, v) for k in range(C) for w, v in ((0, 0), (0, 1), (1, 0))]
                for n, (k, w, v) in enumerate(terms):
                    last = nc.tensor.matmul(result, weights[w][:, k, columns:columns + P], moving(v, k),
                                            start=(n == 0), stop=(n == len(terms) - 1))
                return last

            pe.wait_ge(ident_ready, 1)
            pe.wait_ge(moved, SMALL)
            for c in range(C):
                last = nc.tensor.transpose(ps_rnn[:, c * N:(c + 1) * N], h0_rows[:, c * P:(c + 1) * P],
                                           ident[0:N, 0:N])
            last.then_inc(h0_turned, 1)
            nc.tensor.transpose(ps_turn[1][:, 0:M0 + C], bias_rows[:, :],
                                ident[0:M0 + C, 0:M0 + C]).then_inc(biases_turned, 1)
            pe.wait_ge(biases_read, 1)

            def turn_x(k):
                parity, half = (1 - k.parity, k.half + k.parity)
                pe.wait_ge(x_loaded[parity], 32 * half + 32)
                if k.out:
                    pe.wait_ge(out_copied, 2 * k.b - 2)
                for j in range(J):
                    for c in range(C):
                        last = nc.tensor.transpose(ps_turn[j][:, c * P:(c + 1) * P],
                                                   x_rows[parity][:, j, c * P:(c + 1) * P], ident[:, :])
                    last.then_inc(x_turned, 1)

            def turn_out(k):
                pe.wait_ge(out_summed, BT * (k.b - 1))
                for j in range(J):
                    for c in range(C):
                        last = nc.tensor.transpose(ps_turn[j][:, c * P:(c + 1) * P], outT[:, j, c, :],
                                                   ident[:, :])
                    last.then_inc(out_turned, 1)

            def blocks(k):
                for s in range(BT):
                    t = BT * k.b + s
                    if k.lstm:
                        if k.first and s == 0:
                            pe.wait_ge(w_hi_ready, PIECES_TO["wh0"])
                            pe.wait_ge(w_lo_ready, PIECES_TO["wh0"])
                            pe.wait_ge(h0_hi_ready, 1)
                            pe.wait_ge(h0_lo_ready, 1)
                        else:
                            pe.wait_ge(h_ready, t)
                        if s == 0:
                            pe.wait_ge(proj_read, k.evacuated_before())
                        for result, chunks, done in ((ps_ig, IG_CHUNKS, ig_done), (ps_fo, FO_CHUNKS, fo_done)):
                            for m in chunks:
                                last = products(result[:, m - chunks[0], :], wh0, GATE_COLUMNS[m],
                                                lambda v, c: h_parts[v][:, c * N:(c + 1) * N])
                            last.then_inc(done, 1)
                    if s == 0 and k.out:
                        if k.lstm:
                            pe.wait_ge(x_hi_ready, 2 * k.b + 2)
                        else:
                            pe.wait_ge(out_copied, 2 * k.b - 4)
                        turn_out(k)
                    if s == 0 and k.rnn:
                        if k.rnn_first:
                            pe.wait_ge(w_hi_ready, PIECES_TO["wh1"])
                            pe.wait_ge(w_lo_ready, PIECES_TO["wh1"])
                        pe.wait_ge(y_hi_ready, BT * k.b)
                        pe.wait_ge(y_lo_ready, BT * k.b)
                        for m in range(C):
                            pe.wait_ge(proj_read, k.rnn_chunk(m) - 1)
                            products(ps_proj[m % 2][:, 0:BT * N], wx1, m * P,
                                     lambda v, c: y1_parts[1 - k.parity][v][:, c, :]).then_inc(proj_done, 1)
                    if s == 0 and k.next_x:
                        turn_x(k)
                    if s > 0 and k.next_x:
                        if s == 1:
                            pe.wait_ge(x_lo_ready, 2 * (k.b + 1) + 2)
                            if not k.lstm:
                                pe.wait_ge(w_lo_ready, PIECES_TO["wx0"])
                        for m in CHUNKS_IN_STEP[s]:
                            if k.steady or k.lstm or m >= 2:
                                pe.wait_ge(proj_read, k.lstm_chunk(m) - 1)
                            products(ps_proj[m % 2][:, 0:BT * N], wx0, GATE_COLUMNS[m],
                                     lambda v, c: x_parts[v][:, :, c, :]).then_inc(proj_done, 1)
                    if k.rnn:
                        if k.rnn_first and s == 0:
                            pe.wait_ge(h0_lo_ready, 2)
                        else:
                            pe.wait_ge(rnn_ready, t - BT)
                        for m in range(C):
                            last = products(ps_rnn[:, m * N:(m + 1) * N], wh1, m * P,
                                            lambda v, c: rnn_parts[v][:, c * N:(c + 1) * N])
                        last.then_inc(rnn_done, 1)

            run_blocks(pe, blocks)


def kernel(x, cond_1024, L0_cond_Wx, L0_cond_Wh, L0_cond_b, L1_cond_Wx, L1_cond_Wh, L1_cond_b):
    import numpy as np
    import concourse.bacc as bacc
    from concourse.bass_utils import run_bass_kernel_spmd

    nc = bacc.Bacc("TRN2", target_bir_lowering=False, num_devices=1)
    given = {"x": x, "h0": cond_1024, "Wx0": L0_cond_Wx, "Wh0": L0_cond_Wh, "b0": L0_cond_b,
             "Wx1": L1_cond_Wx, "Wh1": L1_cond_Wh, "b1": L1_cond_b}
    arrays = {f"in_{name}": np.ascontiguousarray(a) for name, a in given.items()}
    aps = [nc.dram_tensor(name, a.shape, F32, kind="ExternalInput").ap() for name, a in arrays.items()]
    out = nc.dram_tensor("out", (N, T, D), F32, kind="ExternalOutput").ap()
    build(nc, *aps, out)
    result = run_bass_kernel_spmd(nc, [arrays], core_ids=[0])
    return result.results[0]["out"]
```

```python
from contextlib import ExitStack

import concourse.bass as bass
import concourse.mybir as mybir
from concourse.alu_op_type import AluOpType as ALU

F32 = mybir.dt.float32
F16 = mybir.dt.float16
U32 = mybir.dt.uint32
ACT = mybir.ActivationFunctionType
AX_X = mybir.AxisListType.X
AX_XY = mybir.AxisListType.XY
ABSMAX = bass.bass_isa.ReduceOp.absmax

P = 128
N = 64
T = 128
D = 512
C = D // P
G = 4
BT = 4
NB = T // BT
J = 2
W = C * N
HIDDEN_SCALE = 2.0 ** 14
EXPONENT_MASK = 0x7F800000
SMALLEST_MAX = 2.0 ** -100

GATE_COLUMNS = [g * D + c * P for g in (0, 3, 1, 2) for c in range(C)]
IG_CHUNKS = range(0, 2 * C)
FO_CHUNKS = range(2 * C, 4 * C)
M0 = G * C
CHUNKS_IN_STEP = [range(0, 0), range(0, 5), range(5, 10), range(10, 16)]


class Block:

    def __init__(self, b, parity, half, known=None):
        self.b, self.parity, self.half = b, parity, half
        k = self.known = known if known is not None else 2
        self.lstm = 0 <= k < NB
        self.rnn = 1 <= k <= NB
        self.rnn_before = 2 <= k <= NB + 1
        self.out = 2 <= k <= NB + 1
        self.next_x = k + 1 < NB
        self.load_x = k + 2 < NB
        self.first = k == 0
        self.rnn_first = k == 1
        self.steady = k >= 2
        self.prologue = k == -1

    def evacuated_before(self):
        if self.steady:
            return 2 * M0 + (M0 + C) * (self.b - 1) - (0 if self.known < NB else M0)
        return {-1: 0, 0: M0, 1: 2 * M0}[self.b]

    def rnn_chunk(self, m):
        return self.evacuated_before() + m

    def lstm_chunk(self, m):
        return self.evacuated_before() + (C if self.rnn else 0) + m


def known_block(b):
    return Block(b, b % 2, b // 2, known=b)


def run_blocks(engine, emit):
    for b in (-1, 0, 1):
        emit(known_block(b))
    with engine.Fori(1, NB // 2 - 1) as i:
        emit(Block(2 * i, 0, i))
        emit(Block(2 * i + 1, 1, i))
    for b in (NB - 2, NB - 1, NB, NB + 1):
        emit(known_block(b))


def build(nc, x, h0, Wx0, Wh0, b0, Wx1, Wh1, b1, out):
    with ExitStack() as ctx:
        def sb(name, shape, dt=F32):
            return ctx.enter_context(nc.sbuf_tensor(name, shape, dt))

        def psum(name, shape):
            return ctx.enter_context(nc.psum_tensor(name, shape, F32))

        def sem(name):
            return ctx.enter_context(nc.semaphore(name))

        wx0 = [sb(f"wx0_{part}", [P, C, G * D], F16) for part in ("hi", "lo")]
        wh0 = [sb(f"wh0_{part}", [P, C, G * D], F16) for part in ("hi", "lo")]
        wx1 = [sb(f"wx1_{part}", [P, C, D], F16) for part in ("hi", "lo")]
        wh1 = [sb(f"wh1_{part}", [P, C, D], F16) for part in ("hi", "lo")]

        arena = sb("arena", [P, 2 * C * G * D])
        stage_wx0 = arena[:, 0:C * G * D].rearrange("p (k n) -> p k n", k=C)
        stage_wh0 = arena[:, C * G * D:2 * C * G * D].rearrange("p (k n) -> p k n", k=C)
        used = [0]

        def from_arena(columns):
            used[0] += columns
            return arena[:, used[0] - columns:used[0]]

        stage_wx1, stage_wh1 = (from_arena(C * D).rearrange("p (k n) -> p k n", k=C) for _ in range(2))
        xz = [sb("xz_even", [P, M0, BT * N]),
              from_arena(M0 * BT * N).rearrange("p (m q) -> p m q", m=M0)]
        assert used[0] == C * G * D
        y1 = [from_arena(BT * W).rearrange("p (q c n) -> p q c n", q=BT, c=C) for _ in range(2)]
        y1_parts = [[from_arena(BT * W // 2).bitcast(F16).rearrange("p (c q) -> p c q", c=C)
                     for _ in range(2)] for _ in range(2)]
        rxz = from_arena(C * BT * N).rearrange("p (m q) -> p m q", m=C)
        outT = from_arena(J * D * 1).rearrange("p (j c q) -> p j c q", j=J, c=C)
        out_rows = from_arena(J * D).rearrange("p (j d) -> p j d", j=J)
        assert used[0] <= 2 * C * G * D

        x_rows = [sb(f"x_rows{i}", [P, J, D]) for i in range(2)]
        xT = [sb(f"xT{i}", [P, J, C, P]) for i in range(2)]
        x_parts = [sb(f"x_{part}", [P, J, C, P], F16) for part in ("hi", "lo")]
        h0_rows = sb("h0_rows", [N, D])
        bias_rows = sb("bias_rows", [M0 + C, P])
        bias = sb("bias", [P, M0 + C])
        ident = sb("ident", [P, P])

        z_lo_ig, z_ig = sb("z_lo_ig", [P, 2 * C, N]), sb("z_ig", [P, 2 * C, N])
        z_lo_fo, z_fo = sb("z_lo_fo", [P, 2 * C, N]), sb("z_fo", [P, 2 * C, N])
        gate_i, gate_g, gate_f, gate_o = (sb(f"gate_{g}", [P, W]) for g in "igfo")
        i_times_g = sb("i_times_g", [P, W])
        f_times_c = sb("f_times_c", [P, W])
        cell = sb("cell", [P, W])
        tanh_cell = sb("tanh_cell", [P, W])
        h_scaled = sb("h_scaled", [P, W])
        h_parts = sb("h_parts", [P, C, 2, N], F16)
        rnn_z_lo, rnn_z = sb("rnn_z_lo", [P, C, N]), sb("rnn_z", [P, C, N])
        rnn_h = sb("rnn_h", [P, W])
        rnn_parts = sb("rnn_parts", [P, C, 2, N], F16)

        x_max_rows = sb("x_max_rows", [P, 1])
        x_max = [sb(f"x_max{i}", [P, 1]) for i in range(2)]
        y_max = sb("y_max", [P, 1])
        inv_x, inv_y = sb("inv_x", [P, 1]), [sb(f"inv_y{i}", [P, 1]) for i in range(2)]
        scale_x, scale_y = sb("scale_x", [P, 1]), [sb(f"scale_y{i}", [P, 1]) for i in range(2)]
        unscale_x = [sb(f"unscale_x{i}", [P, 1]) for i in range(2)]
        unscale_y = sb("unscale_y", [P, 1])
        NAMES = ("wx0", "wh0", "h0", "wx1", "wh1")
        piece_max = {n: sb(f"piece_max_{n}", [P, C]) for n in NAMES}
        part_max = {n: sb(f"part_max_{n}", [P, 1]) for n in NAMES}
        all_max = {n: sb(f"all_max_{n}", [P, 1]) for n in NAMES}
        inv = {n: sb(f"inv_{n}", [P, 1]) for n in NAMES}
        scale = {n: sb(f"scale_{n}", [P, 1]) for n in NAMES}
        unscale_h, unscale_first = sb("unscale_h", [P, 1]), sb("unscale_first", [P, 1])
        rnn_unscale_h, rnn_unscale_first = sb("rnn_unscale_h", [P, 1]), sb("rnn_unscale_first", [P, 1])

        ps_ig = psum("ps_ig", [P, 2 * C, 2, N])
        ps_fo = psum("ps_fo", [P, 2 * C, 2, N])
        ps_rnn = psum("ps_rnn", [P, C, 2, N])
        ps_proj = [psum(f"ps_proj{i}", [P, 512]) for i in range(2)]
        ps_turn = psum("ps_turn", [P, C, P])
        ps_h0 = ps_rnn[:, :, 0, :]
        ps_bias = ps_ig[:, 0, 0, 0:M0 + C]

        w_loaded = {n: [sem(f"w_loaded_{n}{i}") for i in range(C if n in ("wx0", "wh0") else 1)]
                    for n in NAMES if n != "h0"}
        biases_turned, biases_read = sem("biases_turned"), sem("biases_read")
        x_loaded = [sem(f"x_loaded{i}") for i in range(2)]
        moved = sem("moved")
        SMALL = 5 * 16
        ident_zeroed, ident_ready = sem("ident_zeroed"), sem("ident_ready")
        w_pieces_maxed = sem("w_pieces_maxed")
        w_part_maxed = sem("w_part_maxed")
        w_all_maxed = sem("w_all_maxed")
        scale_steps = sem("scale_steps")
        block_steps = sem("block_steps")
        w_scaled = sem("w_scaled")
        w_hi_ready = sem("w_hi_ready")
        w_lo_ready = sem("w_lo_ready")
        h0_turned = sem("h0_turned")
        h0_hi_ready, h0_lo_ready = sem("h0_hi_ready"), sem("h0_lo_ready")
        cell_zeroed = sem("cell_zeroed")
        x_maxed = sem("x_maxed")
        x_all_maxed = sem("x_all_maxed")
        x_scaled = sem("x_scaled")
        x_unscaled = sem("x_unscaled")
        y_unscaled = sem("y_unscaled")
        x_turned = sem("x_turned")
        x_hi_ready = sem("x_hi_ready")
        x_lo_ready = sem("x_lo_ready")
        proj_done, proj_read = sem("proj_done"), sem("proj_read")
        ig_done, fo_done, rnn_done = sem("ig_done"), sem("fo_done"), sem("rnn_done")
        z_lo_ready = sem("z_lo_ready")
        rnn_z_lo_ready = sem("rnn_z_lo_ready")
        z_ig_ready, z_fo_ready = sem("z_ig_ready"), sem("z_fo_ready")
        ig_ready, f_ready, o_ready = sem("ig_ready"), sem("f_ready"), sem("o_ready")
        products_ready = sem("products_ready")
        cell_ready, tanh_cell_ready = sem("cell_ready"), sem("tanh_cell_ready")
        h_scaled_ready, h_hi_ready, h_ready = sem("h_scaled_ready"), sem("h_hi_ready"), sem("h_ready")
        y_ready, y_hi_ready, y_lo_ready = sem("y_ready"), sem("y_hi_ready"), sem("y_lo_ready")
        rnn_z_ready, rnn_tanh_ready = sem("rnn_z_ready"), sem("rnn_tanh_ready")
        rnn_hi_ready, rnn_ready = sem("rnn_hi_ready"), sem("rnn_ready")
        out_summed = sem("out_summed")
        out_turned = sem("out_turned")
        out_copied = sem("out_copied")

        PIECES = {"wx0": C, "wh0": C, "wx1": 1, "wh1": 1}
        PIECES_TO = {"wx0": C, "wh0": 2 * C, "wx1": 2 * C + 1, "wh1": 2 * C + 2}
        STAGE = {"wx0": stage_wx0, "wh0": stage_wh0, "wx1": stage_wx1, "wh1": stage_wh1}
        PARTS = {"wx0": wx0, "wh0": wh0, "wx1": wx1, "wh1": wh1}
        SOURCE = {"wx0": Wx0, "wh0": Wh0, "wx1": Wx1, "wh1": Wh1}

        def piece(name, tensor, n):
            return tensor[:, :, GATE_COLUMNS[C * n]:GATE_COLUMNS[C * n] + D] if PIECES[name] == C else tensor[:, :, :]

        def both_halves(engine, dram, b):
            pairs = dram.rearrange("n (b r) d -> n b (r d)", r=BT // 2)
            starts = [2 * b + tb if isinstance(b, int) else engine.snap(2 * b + tb) for tb in range(2)]
            return [pairs[:, bass.ds(start, 1), :].rearrange("n o e -> n (o e)") for start in starts]

        block = ctx.enter_context(nc.Block())

        @block.sync
        def _(sp):
            def load_x(parity, halves):
                for tb, rows in enumerate(halves):
                    sp.dma_start(x_rows[parity][tb * N:(tb + 1) * N, :, :].rearrange("p j d -> p (j d)"),
                                 rows).then_inc(x_loaded[parity], 16)

            def load_weights(name):
                rows = SOURCE[name].rearrange("(k p) n -> p k n", p=P)
                if len(w_loaded[name]) == 1:
                    sp.dma_start(STAGE[name][:, :, :], rows).then_inc(w_loaded[name][0], 16)
                    return
                for k in range(C):
                    sp.dma_start(STAGE[name][:, k, :], rows[:, k, :]).then_inc(w_loaded[name][k], 16)

            load_x(0, both_halves(sp, x, 0))
            load_weights("wx0")
            load_weights("wh0")

            def blocks(k):
                loads = both_halves(sp, x, k.b + 2) if k.load_x else []
                stores = both_halves(sp, out, k.b - 2) if k.out else []
                if k.load_x:
                    if not k.prologue:
                        sp.wait_ge(x_maxed, k.b + 1)
                        sp.wait_ge(x_turned, 2 * k.b + 2)
                    load_x(k.parity, loads)
                if k.prologue:
                    sp.wait_ge(w_lo_ready, PIECES_TO["wx0"])
                    load_weights("wx1")
                    load_weights("wh1")
                if k.out:
                    sp.wait_ge(out_copied, 2 * k.b - 2)
                    for tb, rows in enumerate(stores):
                        sp.dma_start(rows, out_rows[tb * N:(tb + 1) * N, :, :].rearrange("p j d -> p (j d)")
                                     ).then_inc(moved, 16)

            run_blocks(sp, blocks)
            sp.wait_ge(moved, SMALL + 32 * NB)

        @block.gpsimd
        def _(pool):
            nc.gpsimd.memset(ident[:, :], 0.0).then_inc(ident_zeroed, 1)
            pool.wait_ge(ident_zeroed, 1)
            nc.gpsimd.affine_select(out=ident[:, :], in_=ident[:, :], compare_op=ALU.not_equal, fill=1.0,
                                    base=0, pattern=[[-1, P]], channel_multiplier=1).then_inc(ident_ready, 1)

            def max_of_x(b, parity):
                count = b + 1 if isinstance(b, int) else pool.to_reg(b + 1)
                pool.wait_ge(ident_ready, 1)
                pool.wait_ge(x_maxed, count)
                nc.gpsimd.partition_all_reduce(x_max[parity][:, :], x_max_rows[:, :], P,
                                               ABSMAX).then_inc(x_all_maxed, 1)

            def max_of_weights(name):
                pool.wait_ge(w_part_maxed, NAMES.index(name) + 1)
                nc.gpsimd.partition_all_reduce(all_max[name][:, :], part_max[name][:, :], P,
                                               ABSMAX).then_inc(w_all_maxed, 1)

            max_of_x(0, 0)
            for name in ("wx0", "wh0", "h0"):
                max_of_weights(name)

            def blocks(k):
                if k.first:
                    max_of_weights("wx1")
                    max_of_weights("wh1")
                if k.load_x:
                    max_of_x(k.b + 2, k.parity)

            run_blocks(pool, blocks)

        @block.scalar
        def _(act):
            act.dma_start(h0_rows[:, :], h0).then_inc(moved, 16)
            gates = b0.rearrange("(m p) -> m p", p=P)
            for to, of, count in ((0, 0, C), (C, 3 * C, C), (2 * C, C, 2 * C)):
                act.dma_start(bias_rows[to:to + count, :], gates[of:of + count, :]).then_inc(moved, 16)
            act.dma_start(bias_rows[M0:M0 + C, :], b1.rearrange("(m p) -> m p", p=P)).then_inc(moved, 16)

            def hi_of_weights(name, pieces=None):
                for n in pieces if pieces is not None else range(PIECES[name]):
                    act.wait_ge(w_scaled, NAMES.index(name) + 1)
                    nc.scalar.activation(piece(name, PARTS[name][0], n), piece(name, STAGE[name], n),
                                         ACT.Copy, scale=scale[name][:, :]).then_inc(w_hi_ready, 1)

            def read_lstm_chunk(k, m):
                act.wait_ge(proj_done, k.lstm_chunk(m) + 1)
                nc.scalar.activation(xz[1 - k.parity][:, m, :], ps_proj[m % 2][:, 0:BT * N], ACT.Identity,
                                     bias=bias[:, m:m + 1],
                                     scale=unscale_x[1 - k.parity][:, :]).then_inc(proj_read, 1)

            def read_rnn_chunk(k, m):
                act.wait_ge(proj_done, k.rnn_chunk(m) + 1)
                nc.scalar.activation(rxz[:, m, :], ps_proj[m % 2][:, 0:BT * N], ACT.Identity,
                                     bias=bias[:, M0 + m:M0 + m + 1],
                                     scale=unscale_y[:, :]).then_inc(proj_read, 1)

            def read_x(b, parity, j):
                act.wait_ge(x_scaled, b + 1)
                act.wait_ge(x_turned, 2 * b + j + 1)
                nc.scalar.activation(xT[parity][:, j, :, :], ps_turn[:, :, :], ACT.Copy)
                nc.scalar.activation(x_parts[0][:, j, :, :], ps_turn[:, :, :], ACT.Copy,
                                     scale=scale_x[:, :]).then_inc(x_hi_ready, 1)

            def read_out(k, j):
                if j == 0:
                    act.wait_ge(moved, SMALL + 32 * (k.b - 2))
                act.wait_ge(out_turned, 2 * (k.b - 2) + j + 1)
                nc.scalar.activation(out_rows[:, j, :], ps_turn[:, :, :].rearrange("p c q -> p (c q)"),
                                     ACT.Copy).then_inc(out_copied, 1)

            def as_chunks(gate):
                return gate[:, :].rearrange("p (c n) -> p c n", c=C)

            read_x(0, 0, 0)
            act.wait_ge(biases_turned, 1)
            nc.scalar.activation(bias[:, :], ps_bias, ACT.Copy).then_inc(biases_read, 1)
            read_x(0, 0, 1)
            hi_of_weights("wx0")

            def blocks(k):
                for s in range(BT):
                    t = BT * k.b + s
                    j, tb = s % 2, s // 2
                    if s == 0:
                        chunks = [(read_rnn_chunk, m) for m in range(C)] if k.rnn else []
                    else:
                        chunks = [(read_lstm_chunk, m) for m in CHUNKS_IN_STEP[s]] if k.next_x else []

                    def read_chunks(count):
                        for read, m in chunks[:count]:
                            read(k, m)
                        del chunks[:count]

                    if k.rnn_before if s == 0 else k.rnn:
                        act.wait_ge(rnn_z_ready, t - BT)
                        if k.steady or s >= 2:
                            act.wait_ge(out_summed, t - 1 - BT)
                            act.wait_ge(rnn_ready, t - 1 - BT)
                        nc.scalar.activation(as_chunks(rnn_h), rnn_z[:, :, :],
                                             ACT.Tanh).then_inc(rnn_tanh_ready, 1)
                    if k.lstm:
                        act.wait_ge(z_ig_ready, t + 1)
                        nc.scalar.activation(as_chunks(gate_i), z_ig[:, 0:C, :], ACT.Sigmoid)
                        nc.scalar.activation(as_chunks(gate_g), z_ig[:, C:2 * C, :],
                                             ACT.Tanh).then_inc(ig_ready, 1)
                    if s < 2 and k.out:
                        read_out(k, s)
                    if s == 0 and k.rnn:
                        act.wait_ge(y_unscaled, k.b)
                        if k.rnn_before:
                            act.wait_ge(rnn_z_ready, BT * (k.b - 1))
                    if s == 1 and k.next_x:
                        act.wait_ge(x_unscaled, k.b + 2)
                    if k.lstm:
                        if s > 0:
                            read_chunks(1)
                        act.wait_ge(z_fo_ready, t + 1)
                        nc.scalar.activation(as_chunks(gate_f), z_fo[:, 0:C, :], ACT.Sigmoid).then_inc(f_ready, 1)
                        nc.scalar.activation(as_chunks(gate_o), z_fo[:, C:2 * C, :],
                                             ACT.Sigmoid).then_inc(o_ready, 1)
                        read_chunks(1)
                        act.wait_ge(cell_ready, t + 1)
                        nc.scalar.activation(tanh_cell[:, :], cell[:, :], ACT.Tanh).then_inc(tanh_cell_ready, 1)
                        read_chunks(2)
                        act.wait_ge(y_ready, t + 1)
                        nc.scalar.activation(
                            y1_parts[k.parity][0][:, :, (2 * j + tb) * N:(2 * j + tb + 1) * N],
                            y1[k.parity][:, 2 * j + tb, :, :], ACT.Copy,
                            scale=scale_y[k.parity][:, :]).then_inc(y_hi_ready, 1)
                    if k.prologue and s == BT - 1:
                        read_chunks(3)
                        for n in range(C):
                            hi_of_weights("wh0", [n])
                            read_chunks(1)
                        act.wait_ge(w_scaled, NAMES.index("h0") + 1)
                        for parts in (h_parts, rnn_parts):
                            last = nc.scalar.activation(parts[:, :, 0, :], ps_h0, ACT.Copy,
                                                        scale=scale["h0"][:, :])
                        last.then_inc(h0_hi_ready, 1)
                    read_chunks(len(chunks))
                    if s == 0 and k.next_x and not k.prologue:
                        read_x(k.b + 1, 1 - k.parity, 1)
                    if k.first and s >= 2:
                        hi_of_weights(("wx1", "wh1")[s - 2])
                    if s == BT - 1 and k.load_x:
                        read_x(k.b + 2, k.parity, 0)

            run_blocks(act, blocks)

        @block.vector
        def _(dve):
            own = [0]

            def scale_step(instruction):
                own[0] += 1
                instruction.then_inc(scale_steps, 1)
                dve.wait_ge(scale_steps, own[0])

            def power_below(result, maximum):
                bits = result.bitcast(U32)
                yield nc.vector.tensor_scalar(result, maximum, SMALLEST_MAX, None, ALU.max)
                yield nc.vector.tensor_scalar(bits, bits, EXPONENT_MASK, None, ALU.bitwise_and)
                yield nc.vector.tensor_scalar(result, result, 1.0 / HIDDEN_SCALE, None, ALU.mult)

            maxed = [0]

            def max_of_loaded(name, n):
                dve.wait_ge(w_loaded[name][n], 16)
                count = len(w_loaded[name])
                source = STAGE[name][:, n, :] if count == C else STAGE[name].rearrange("p k n -> p (k n)")
                result = piece_max[name][:, n:n + 1] if count == C else part_max[name][:, :]
                last = nc.vector.tensor_reduce(result, source, AX_X, ALU.max, apply_absolute_value=True)
                if count == 1:
                    last.then_inc(w_part_maxed, 1)
                elif n == C - 1:
                    maxed[0] += 1
                    last.then_inc(w_pieces_maxed, 1)
                    dve.wait_ge(w_pieces_maxed, maxed[0])
                    nc.vector.tensor_reduce(part_max[name][:, :], piece_max[name][:, :], AX_X,
                                            ALU.max).then_inc(w_part_maxed, 1)

            def scale_of_weights(name):
                dve.wait_ge(w_all_maxed, NAMES.index(name) + 1)
                for step in power_below(inv[name][:, :], all_max[name][:, :]):
                    scale_step(step)
                nc.vector.reciprocal(scale[name][:, :], inv[name][:, :]).then_inc(w_scaled, 1)

            def lo_of_weights(name, n):
                dve.wait_ge(w_hi_ready, PIECES_TO[name] - PIECES[name] + n + 1)
                a, h, l = (piece(name, v, n) for v in (STAGE[name], PARTS[name][0], PARTS[name][1]))
                nc.vector.scalar_tensor_tensor(l, a, scale[name][:, :], h, ALU.mult,
                                               ALU.subtract).then_inc(w_lo_ready, 1)

            def max_of_x(b, parity, half):
                dve.wait_ge(x_loaded[parity], 32 * half + 32)
                nc.vector.tensor_reduce(x_max_rows[:, :], x_rows[parity][:, :, :].rearrange("p j d -> p (j d)"),
                                        AX_X, ALU.max, apply_absolute_value=True).then_inc(x_maxed, 1)

            def scales_of_block(b, parity):
                dve.wait_ge(x_all_maxed, b + 1)
                nc.vector.tensor_scalar(y_max[:, :], x_max[parity][:, :], 1.0, None, ALU.add
                                        ).then_inc(block_steps, 1)
                count = 7 * b + 1
                for maximum, result in ((x_max[parity], inv_x), (y_max, inv_y[parity])):
                    for step in power_below(result[:, :], maximum[:, :]):
                        step.then_inc(block_steps, 1)
                        count = count + 1
                        dve.wait_ge(block_steps, count)
                nc.vector.reciprocal(scale_x[:, :], inv_x[:, :])
                nc.vector.reciprocal(scale_y[parity][:, :], inv_y[parity][:, :]).then_inc(x_scaled, 1)

            def unscale_of_x(parity):
                nc.vector.tensor_tensor(unscale_x[parity][:, :], inv_x[:, :], inv["wx0"][:, :],
                                        ALU.mult).then_inc(x_unscaled, 1)

            def lo_of_x(b, parity, j):
                dve.wait_ge(x_hi_ready, 2 * b + j + 1)
                nc.vector.scalar_tensor_tensor(
                    x_parts[1][:, j, :, :].rearrange("p c q -> p (c q)"),
                    xT[parity][:, j, :, :].rearrange("p c q -> p (c q)"), scale_x[:, :],
                    x_parts[0][:, j, :, :].rearrange("p c q -> p (c q)"), ALU.mult,
                    ALU.subtract).then_inc(x_lo_ready, 1)

            def add_products(z, z_lo, products, unscale, inputs, lo_ready, count, ready):
                nc.vector.scalar_tensor_tensor(z_lo[:, :, :], products[:, :, 1, :], unscale[:, :], inputs,
                                               ALU.mult, ALU.add).then_inc(lo_ready, 1)
                dve.wait_ge(lo_ready, count)
                nc.vector.scalar_tensor_tensor(z[:, :, :], products[:, :, 0, :], unscale[:, :],
                                               z_lo[:, :, :], ALU.mult, ALU.add).then_inc(ready, 1)

            def as_chunks(state):
                return state[:, :].rearrange("p (c n) -> p c n", c=C)

            def lstm_step(k, s):
                t = BT * k.b + s
                j, tb = s % 2, s // 2
                q = 2 * j + tb
                here = slice(q * N, (q + 1) * N)
                unscale = unscale_first if k.first and s == 0 else unscale_h
                dve.wait_ge(ig_done, t + 1)
                add_products(z_ig, z_lo_ig, ps_ig, unscale, xz[k.parity][:, 0:2 * C, here],
                             z_lo_ready, 2 * t + 1, z_ig_ready)
                dve.wait_ge(ig_ready, t + 1)
                nc.vector.tensor_tensor(i_times_g[:, :], gate_i[:, :], gate_g[:, :],
                                        ALU.mult).then_inc(products_ready, 1)
                dve.wait_ge(fo_done, t + 1)
                add_products(z_fo, z_lo_fo, ps_fo, unscale, xz[k.parity][:, 2 * C:4 * C, here],
                             z_lo_ready, 2 * t + 2, z_fo_ready)
                dve.wait_ge(f_ready, t + 1)
                nc.vector.tensor_tensor(f_times_c[:, :], gate_f[:, :], cell[:, :],
                                        ALU.mult).then_inc(products_ready, 1)
                dve.wait_ge(products_ready, 2 * t + 2)
                nc.vector.tensor_tensor(cell[:, :], f_times_c[:, :], i_times_g[:, :],
                                        ALU.add).then_inc(cell_ready, 1)
                dve.wait_ge(o_ready, t + 1)
                dve.wait_ge(tanh_cell_ready, t + 1)
                nc.vector.scalar_tensor_tensor(h_scaled[:, :], gate_o[:, :], HIDDEN_SCALE, tanh_cell[:, :],
                                               ALU.mult, ALU.mult).then_inc(h_scaled_ready, 1)
                dve.wait_ge(h_scaled_ready, t + 1)
                nc.vector.tensor_copy(h_parts[:, :, 0, :], as_chunks(h_scaled)).then_inc(h_hi_ready, 1)
                dve.wait_ge(h_hi_ready, t + 1)
                nc.vector.tensor_tensor(h_parts[:, :, 1, :], as_chunks(h_scaled), h_parts[:, :, 0, :],
                                        ALU.subtract).then_inc(h_ready, 1)
                nc.vector.scalar_tensor_tensor(
                    y1[k.parity][:, q, :, :], as_chunks(h_scaled),
                    1.0 / HIDDEN_SCALE, xT[k.parity][:, j, :, tb * N:(tb + 1) * N], ALU.mult,
                    ALU.add).then_inc(y_ready, 1)
                dve.wait_ge(y_hi_ready, t + 1)
                nc.vector.scalar_tensor_tensor(
                    y1_parts[k.parity][1][:, :, here], y1[k.parity][:, q, :, :], scale_y[k.parity][:, :],
                    y1_parts[k.parity][0][:, :, here], ALU.mult, ALU.subtract).then_inc(y_lo_ready, 1)

            def rnn_step(k, s):
                r = BT * k.b + s - 1 - BT
                j, tb = (s - 1) % BT % 2, (s - 1) % BT // 2
                q = 2 * j + tb
                unscale = rnn_unscale_first if k.rnn_first and s == 1 else rnn_unscale_h
                if s == 1:
                    dve.wait_ge(proj_read, k.rnn_chunk(C))
                dve.wait_ge(rnn_done, r + 1)
                add_products(rnn_z, rnn_z_lo, ps_rnn, unscale, rxz[:, :, q * N:(q + 1) * N],
                             rnn_z_lo_ready, r + 1, rnn_z_ready)
                dve.wait_ge(rnn_tanh_ready, r + 1)
                nc.vector.tensor_scalar(rnn_parts[:, :, 0, :], as_chunks(rnn_h), HIDDEN_SCALE, None,
                                        ALU.mult).then_inc(rnn_hi_ready, 1)
                dve.wait_ge(rnn_hi_ready, r + 1)
                nc.vector.scalar_tensor_tensor(rnn_parts[:, :, 1, :], as_chunks(rnn_h), HIDDEN_SCALE,
                                               rnn_parts[:, :, 0, :], ALU.mult,
                                               ALU.subtract).then_inc(rnn_ready, 1)
                nc.vector.tensor_tensor(
                    outT[:, j, :, tb * N:(tb + 1) * N], y1[k.parity if s == 0 else 1 - k.parity][:, q, :, :],
                    as_chunks(rnn_h), ALU.add).then_inc(out_summed, 1)

            nc.vector.memset(cell[:, :], 0.0).then_inc(cell_zeroed, 1)
            max_of_x(0, 0, 0)
            scales_of_block(0, 0)
            lo_of_x(0, 0, 0)
            lo_of_x(0, 0, 1)
            for n in range(C):
                max_of_loaded("wx0", n)
            scale_of_weights("wx0")
            unscale_of_x(0)
            for n in range(C):
                lo_of_weights("wx0", n)
                max_of_loaded("wh0", n)
            dve.wait_ge(h0_turned, 1)
            nc.vector.tensor_reduce(part_max["h0"][:, :], ps_h0, AX_XY, ALU.max,
                                    apply_absolute_value=True).then_inc(w_part_maxed, 1)
            for name in ("wh0", "h0"):
                scale_of_weights(name)
            nc.vector.tensor_scalar(unscale_h[:, :], inv["wh0"][:, :], 1.0 / HIDDEN_SCALE, None, ALU.mult)
            nc.vector.tensor_tensor(unscale_first[:, :], inv["wh0"][:, :], inv["h0"][:, :], ALU.mult)
            for n in range(C):
                lo_of_weights("wh0", n)
            dve.wait_ge(h0_hi_ready, 1)
            for parts in (h_parts, rnn_parts):
                nc.vector.scalar_tensor_tensor(parts[:, :, 1, :], ps_h0, scale["h0"][:, :],
                                               parts[:, :, 0, :], ALU.mult,
                                               ALU.subtract).then_inc(h0_lo_ready, 1)
            dve.wait_ge(cell_zeroed, 1)

            def second_layer_weights(s):
                if s < 2:
                    max_of_loaded(("wx1", "wh1")[s], 0)
                if s == 1:
                    for name in ("wx1", "wh1"):
                        scale_of_weights(name)
                    nc.vector.tensor_scalar(rnn_unscale_h[:, :], inv["wh1"][:, :], 1.0 / HIDDEN_SCALE, None,
                                            ALU.mult)
                    nc.vector.tensor_tensor(rnn_unscale_first[:, :], inv["wh1"][:, :], inv["h0"][:, :],
                                            ALU.mult)
                if s >= 2:
                    lo_of_weights(("wx1", "wh1")[s - 2], 0)

            def blocks(k):
                for s in range(BT):
                    if s < 2 and k.next_x and not k.prologue:
                        lo_of_x(k.b + 1, 1 - k.parity, s)
                    if k.rnn_before if s == 0 else k.rnn:
                        rnn_step(k, s)
                    if k.lstm:
                        lstm_step(k, s)
                    if k.first:
                        second_layer_weights(s)
                    if s == 2 and k.load_x:
                        dve.wait_ge(x_all_maxed, k.b + 2)
                        max_of_x(k.b + 2, k.parity, k.half + 1)
                    if s == BT - 1 and k.lstm:
                        nc.vector.tensor_tensor(unscale_y[:, :], inv_y[k.parity][:, :], inv["wx1"][:, :],
                                                ALU.mult).then_inc(y_unscaled, 1)
                    if s == BT - 1 and k.load_x:
                        scales_of_block(k.b + 2, k.parity)
                        unscale_of_x(k.parity)

            run_blocks(dve, blocks)

        @block.tensor
        def _(pe):
            def input_products(result, weights, columns, moving):
                terms = [(k, w, v) for k in range(C) for w, v in ((0, 0), (0, 1), (1, 0))]
                for n, (k, w, v) in enumerate(terms):
                    last = nc.tensor.matmul(result, weights[w][:, k, columns:columns + P], moving(v, k),
                                            start=(n == 0), stop=(n == len(terms) - 1))
                return last

            def recurrent_products(result, weights, columns, parts):
                for k in range(C):
                    hi, lo = (w[:, k, columns:columns + P] for w in weights)
                    both, upper = parts[:, k, :, :].rearrange("p v n -> p (v n)"), parts[:, k, 0, :]
                    whole, first = result.rearrange("p v n -> p (v n)"), result[:, 0, :]
                    if k < C - 1:
                        nc.tensor.matmul(whole, hi, both, start=(k == 0), stop=False)
                        nc.tensor.matmul(first, lo, upper, start=False, stop=False)
                    else:
                        nc.tensor.matmul(first, lo, upper, start=False, stop=False)
                        last = nc.tensor.matmul(whole, hi, both, start=False, stop=True)
                return last

            def turn_x(b, parity, half, j):
                if j == 0:
                    pe.wait_ge(x_loaded[parity], 32 * half + 32)
                for c in range(C):
                    last = nc.tensor.transpose(ps_turn[:, c, :], x_rows[parity][:, j, c * P:(c + 1) * P],
                                               ident[:, :])
                last.then_inc(x_turned, 1)

            def turn_out(k, j):
                pe.wait_ge(out_summed, BT * (k.b - 1) - 1 + j)
                for c in range(C):
                    last = nc.tensor.transpose(ps_turn[:, c, :], outT[:, j, c, :], ident[:, :])
                last.then_inc(out_turned, 1)

            pe.wait_ge(ident_ready, 1)
            turn_x(0, 0, 0, 0)
            pe.wait_ge(moved, SMALL)
            for c in range(C):
                last = nc.tensor.transpose(ps_h0[:, c, :], h0_rows[:, c * P:(c + 1) * P], ident[0:N, 0:N])
            last.then_inc(h0_turned, 1)
            nc.tensor.transpose(ps_bias, bias_rows[:, :],
                                ident[0:M0 + C, 0:M0 + C]).then_inc(biases_turned, 1)
            pe.wait_ge(x_hi_ready, 1)
            turn_x(0, 0, 0, 1)

            def blocks(k):
                for s in range(BT):
                    t = BT * k.b + s
                    if k.lstm:
                        if k.first and s == 0:
                            pe.wait_ge(h0_hi_ready, 1)
                            pe.wait_ge(h0_lo_ready, 1)
                            pe.wait_ge(biases_read, 1)
                        else:
                            pe.wait_ge(h_ready, t)
                        if s == 0:
                            pe.wait_ge(proj_read, k.evacuated_before())
                        for half, (result, chunks, done) in enumerate(((ps_ig, IG_CHUNKS, ig_done),
                                                                       (ps_fo, FO_CHUNKS, fo_done))):
                            if k.first and s == 0:
                                pe.wait_ge(w_lo_ready, PIECES_TO["wx0"] + 2 * half + 2)
                            for m in chunks:
                                last = recurrent_products(result[:, m - chunks[0], :, :], wh0,
                                                          GATE_COLUMNS[m], h_parts)
                            last.then_inc(done, 1)
                    if s == 0 and k.out:
                        if k.next_x:
                            pe.wait_ge(x_hi_ready, 2 * k.b + 3)
                        else:
                            pe.wait_ge(out_copied, 2 * k.b - 4)
                        turn_out(k, 0)
                    if s == 0 and k.rnn:
                        if k.rnn_first:
                            pe.wait_ge(w_lo_ready, PIECES_TO["wh1"])
                        pe.wait_ge(y_hi_ready, BT * k.b)
                        pe.wait_ge(y_lo_ready, BT * k.b)
                        for m in range(C):
                            pe.wait_ge(proj_read, k.rnn_chunk(m) - 1)
                            input_products(ps_proj[m % 2][:, 0:BT * N], wx1, m * P,
                                           lambda v, c: y1_parts[1 - k.parity][v][:, c, :]
                                           ).then_inc(proj_done, 1)
                    if s == 0 and k.next_x and not k.prologue:
                        if k.out:
                            pe.wait_ge(out_copied, 2 * k.b - 3)
                        else:
                            pe.wait_ge(x_hi_ready, 2 * k.b + 3)
                        turn_x(k.b + 1, 1 - k.parity, k.half + k.parity, 1)
                    if s == 1 and k.out:
                        if k.next_x:
                            pe.wait_ge(x_hi_ready, 2 * k.b + 4)
                        else:
                            pe.wait_ge(out_copied, 2 * k.b - 3)
                        turn_out(k, 1)
                    if s > 0 and k.next_x:
                        if s == 1:
                            pe.wait_ge(x_lo_ready, 2 * (k.b + 1) + 2)
                        for m in CHUNKS_IN_STEP[s]:
                            if k.prologue and m % C == 0:
                                pe.wait_ge(w_lo_ready, m // C + 1)
                            if not k.prologue or m >= 2:
                                pe.wait_ge(proj_read, k.lstm_chunk(m) - 1)
                            input_products(ps_proj[m % 2][:, 0:BT * N], wx0, GATE_COLUMNS[m],
                                           lambda v, c: x_parts[v][:, :, c, :]).then_inc(proj_done, 1)
                    if s == BT - 1 and k.load_x:
                        if k.out:
                            pe.wait_ge(out_copied, 2 * k.b - 2)
                        else:
                            pe.wait_ge(x_hi_ready, 2 * k.b + 4)
                        turn_x(k.b + 2, k.parity, k.half + 1, 0)
                    if k.rnn:
                        if k.rnn_first and s == 0:
                            pe.wait_ge(h0_lo_ready, 2)
                        else:
                            pe.wait_ge(rnn_ready, t - BT)
                        for m in range(C):
                            last = recurrent_products(ps_rnn[:, m, :, :], wh1, m * P, rnn_parts)
                        last.then_inc(rnn_done, 1)

            run_blocks(pe, blocks)


def kernel(x, cond_1024, L0_cond_Wx, L0_cond_Wh, L0_cond_b, L1_cond_Wx, L1_cond_Wh, L1_cond_b):
    import numpy as np
    import concourse.bacc as bacc
    from concourse.bass_utils import run_bass_kernel_spmd

    nc = bacc.Bacc("TRN2", target_bir_lowering=False, num_devices=1)
    given = {"x": x, "h0": cond_1024, "Wx0": L0_cond_Wx, "Wh0": L0_cond_Wh, "b0": L0_cond_b,
             "Wx1": L1_cond_Wx, "Wh1": L1_cond_Wh, "b1": L1_cond_b}
    arrays = {f"in_{name}": np.ascontiguousarray(a) for name, a in given.items()}
    aps = [nc.dram_tensor(name, a.shape, F32, kind="ExternalInput").ap() for name, a in arrays.items()]
    out = nc.dram_tensor("out", (N, T, D), F32, kind="ExternalOutput").ap()
    build(nc, *aps, out)
    result = run_bass_kernel_spmd(nc, [arrays], core_ids=[0])
    return result.results[0]["out"]
```

```python
from contextlib import ExitStack

import concourse.bass as bass
import concourse.mybir as mybir
from concourse.alu_op_type import AluOpType as ALU

F32 = mybir.dt.float32
F16 = mybir.dt.float16
U32 = mybir.dt.uint32
ACT = mybir.ActivationFunctionType
AX_X = mybir.AxisListType.X
AX_XY = mybir.AxisListType.XY
ABSMAX = bass.bass_isa.ReduceOp.absmax

P = 128
N = 64
T = 128
D = 512
C = D // P
G = 4
BT = 4
NB = T // BT
J = 2
W = C * N
HIDDEN_SCALE = 2.0 ** 14
EXPONENT_MASK = 0x7F800000
SMALLEST_MAX = 2.0 ** -100

GATE_COLUMNS = [g * D + c * P for g in (0, 3, 1, 2) for c in range(C)]
IG_CHUNKS = range(0, 2 * C)
FO_CHUNKS = range(2 * C, 4 * C)
M0 = G * C
CHUNKS_IN_STEP = [range(0, 0), range(0, 5), range(5, 10), range(10, 16)]
CHUNKS_IN_FIRST_STEPS = [range(0, 4), range(4, 8), range(8, 12), range(12, 16)]


class Block:

    def __init__(self, b, parity, half, known=None):
        self.b, self.parity, self.half = b, parity, half
        k = self.known = known if known is not None else 2
        self.lstm = k >= 0
        self.rnn = k >= 1
        self.rnn_before = k >= 2
        self.out = k >= 2
        self.next_x = k + 1 < NB
        self.load_x = k + 2 < NB
        self.first = k == 0
        self.rnn_first = k == 1
        self.last = k == NB - 1
        self.steady = k >= 2
        self.prologue = k == -1
        self.chunks_in_step = CHUNKS_IN_FIRST_STEPS if self.first else CHUNKS_IN_STEP

    def evacuated_before(self):
        if self.steady:
            return 2 * M0 + (M0 + C) * (self.b - 1)
        return {-1: 0, 0: M0, 1: 2 * M0}[self.b]

    def late_rnn_step(self, s):
        return BT * self.b + s - BT + (s if self.last else 0)

    def early_rnn_step(self, s):
        return self.late_rnn_step(s - 1) if s > 0 else BT * self.b - 1 - BT

    def middle_rnn_step(self, s):
        return self.late_rnn_step(s) - 1

    def rnn_chunk(self, m):
        return self.evacuated_before() + m

    def lstm_chunk(self, m):
        return self.evacuated_before() + (C if self.rnn else 0) + m


def known_block(b):
    return Block(b, b % 2, b // 2, known=b)


def place(s):
    s = s % BT
    j, tb = s % J, s // J
    return j, tb, J * j + tb


def run_blocks(engine, emit):
    for b in (-1, 0, 1):
        emit(known_block(b))
    with engine.Fori(1, NB // 2 - 1) as i:
        emit(Block(2 * i, 0, i))
        emit(Block(2 * i + 1, 1, i))
    for b in (NB - 2, NB - 1):
        emit(known_block(b))


def build(nc, x, h0, Wx0, Wh0, b0, Wx1, Wh1, b1, out):
    with ExitStack() as ctx:
        def sb(name, shape, dt=F32):
            return ctx.enter_context(nc.sbuf_tensor(name, shape, dt))

        def psum(name, shape):
            return ctx.enter_context(nc.psum_tensor(name, shape, F32))

        def sem(name):
            return ctx.enter_context(nc.semaphore(name))

        wx0 = [sb(f"wx0_{part}", [P, C, G * D], F16) for part in ("hi", "lo")]
        wh0 = [sb(f"wh0_{part}", [P, C, G * D], F16) for part in ("hi", "lo")]
        wx1 = [sb(f"wx1_{part}", [P, C, D], F16) for part in ("hi", "lo")]
        wh1 = [sb(f"wh1_{part}", [P, C, D], F16) for part in ("hi", "lo")]

        arena = sb("arena", [P, 2 * C * G * D])
        stage_wx0 = arena[:, 0:C * G * D].rearrange("p (k n) -> p k n", k=C)
        stage_wh0 = arena[:, C * G * D:2 * C * G * D].rearrange("p (k n) -> p k n", k=C)
        used = [0]

        def from_arena(columns):
            used[0] += columns
            return arena[:, used[0] - columns:used[0]]

        stage_wx1, stage_wh1 = (from_arena(C * D).rearrange("p (k n) -> p k n", k=C) for _ in range(2))
        xz = [sb("xz_even", [P, M0, BT * N]),
              from_arena(M0 * BT * N).rearrange("p (m q) -> p m q", m=M0)]
        assert used[0] == C * G * D
        y1 = [from_arena(BT * W).rearrange("p (q c n) -> p q c n", q=BT, c=C) for _ in range(2)]
        y1_parts = [[from_arena(BT * W // 2).bitcast(F16).rearrange("p (c q) -> p c q", c=C)
                     for _ in range(2)] for _ in range(2)]
        rxz = from_arena(C * BT * N).rearrange("p (m q) -> p m q", m=C)
        outT = from_arena(J * D * 1).rearrange("p (j c q) -> p j c q", j=J, c=C)
        out_rows = from_arena(J * D).rearrange("p (j d) -> p j d", j=J)
        assert used[0] <= 2 * C * G * D

        x_rows = [sb(f"x_rows{i}", [P, J, D]) for i in range(2)]
        xT = [sb(f"xT{i}", [P, J, C, P]) for i in range(2)]
        x_parts = [sb(f"x_{part}", [P, J, C, P], F16) for part in ("hi", "lo")]
        h0_rows = sb("h0_rows", [N, D])
        bias_rows = sb("bias_rows", [M0 + C, P])
        bias = sb("bias", [P, M0 + C])
        ident = sb("ident", [P, P])

        z_lo_ig, z_ig = sb("z_lo_ig", [P, 2 * C, N]), sb("z_ig", [P, 2 * C, N])
        z_lo_fo, z_fo = sb("z_lo_fo", [P, 2 * C, N]), sb("z_fo", [P, 2 * C, N])
        gate_i, gate_g, gate_f, gate_o = (sb(f"gate_{g}", [P, W]) for g in "igfo")
        i_times_g = sb("i_times_g", [P, W])
        f_times_c = sb("f_times_c", [P, W])
        cell = sb("cell", [P, W])
        tanh_cell = sb("tanh_cell", [P, W])
        h_scaled = sb("h_scaled", [P, W])
        h_parts = sb("h_parts", [P, C, 2, N], F16)
        rnn_z_lo, rnn_z = sb("rnn_z_lo", [P, C, N]), sb("rnn_z", [P, C, N])
        rnn_h = sb("rnn_h", [P, W])
        rnn_parts = sb("rnn_parts", [P, C, 2, N], F16)

        x_max_rows = sb("x_max_rows", [P, 1])
        x_max = [sb(f"x_max{i}", [P, 1]) for i in range(2)]
        y_max = sb("y_max", [P, 1])
        inv_x, inv_y = sb("inv_x", [P, 1]), [sb(f"inv_y{i}", [P, 1]) for i in range(2)]
        scale_x, scale_y = sb("scale_x", [P, 1]), [sb(f"scale_y{i}", [P, 1]) for i in range(2)]
        unscale_x = [sb(f"unscale_x{i}", [P, 2]) for i in range(2)]
        unscale_y = sb("unscale_y", [P, 1])
        NAMES = ("h0", "wx0_ig", "wx0_fo", "wh0_ig", "wh0_fo", "wx1", "wh1")
        HALVES = NAMES[1:5]
        MAXIMA = {n: 1 if n == "h0" else 2 if n in HALVES else C for n in NAMES}
        part_max = {n: sb(f"part_max_{n}", [P, MAXIMA[n]]) for n in NAMES}
        all_max = {n: sb(f"all_max_{n}", [P, MAXIMA[n]]) for n in NAMES}
        all_max_whole = sb("all_max_whole", [P, 1])
        inv_all, scale_all = sb("inv_all", [P, len(NAMES)]), sb("scale_all", [P, len(NAMES)])
        inv = {n: inv_all[:, i:i + 1] for i, n in enumerate(NAMES)}
        scale = {n: scale_all[:, i:i + 1] for i, n in enumerate(NAMES)}
        inv_wx0, inv_wh0 = inv_all[:, 1:3], inv_all[:, 3:5]
        unscale_h, unscale_first = sb("unscale_h", [P, 2]), sb("unscale_first", [P, 2])
        rnn_unscale_h, rnn_unscale_first = sb("rnn_unscale_h", [P, 1]), sb("rnn_unscale_first", [P, 1])

        ps_ig = psum("ps_ig", [P, 2 * C, 2, N])
        ps_fo = psum("ps_fo", [P, 2 * C, 2, N])
        ps_rnn = psum("ps_rnn", [P, C, 2, N])
        ps_proj = [psum(f"ps_proj{i}", [P, 512]) for i in range(2)]
        ps_turn = psum("ps_turn", [P, C, P])
        prologue_banks = ps_proj + [ps_fo[:, half * C:(half + 1) * C, :, :].rearrange("p m v n -> p (m v n)")
                                    for half in range(2)]
        ps_h0 = ps_rnn[:, :, 0, :]
        ps_bias = ps_ig[:, 0, 0, 0:M0 + C]

        PIECES_TO = {"wx0": G, "wh0": 2 * G, "wx1": 2 * G + C, "wh1": 2 * G + 2 * C}
        LOADS = {"wx0": G, "wh0": G, "wx1": 1, "wh1": 1}
        w_loaded = {n: [sem(f"w_loaded_{n}{i}") for i in range(LOADS[n])]
                    for n in LOADS}
        h0_loaded = sem("h0_loaded")
        biases_turned, biases_read = sem("biases_turned"), sem("biases_read")
        x_loaded = [sem(f"x_loaded{i}") for i in range(2)]
        moved = sem("moved")
        SMALL = 4 * 16
        ident_zeroed, ident_ready = sem("ident_zeroed"), sem("ident_ready")
        w_part_maxed = sem("w_part_maxed")
        w_all_maxed = sem("w_all_maxed")
        scale_steps = sem("scale_steps")
        block_steps = sem("block_steps")
        w_scaled = sem("w_scaled")
        w_hi_ready = sem("w_hi_ready")
        w_lo_ready = sem("w_lo_ready")
        h0_turned = sem("h0_turned")
        h0_hi_ready, h0_lo_ready = sem("h0_hi_ready"), sem("h0_lo_ready")
        cell_zeroed = sem("cell_zeroed")
        x_maxed = sem("x_maxed")
        x_all_maxed = sem("x_all_maxed")
        x_scaled = sem("x_scaled")
        x_unscaled = sem("x_unscaled")
        y_unscaled = sem("y_unscaled")
        x_turned = sem("x_turned")
        x_hi_ready = sem("x_hi_ready")
        x_lo_ready = sem("x_lo_ready")
        proj_done, proj_read = sem("proj_done"), sem("proj_read")
        last_proj_done, last_proj_read = sem("last_proj_done"), sem("last_proj_read")
        ig_done, fo_done, rnn_done = sem("ig_done"), sem("fo_done"), sem("rnn_done")
        z_lo_ready = sem("z_lo_ready")
        rnn_z_lo_ready = sem("rnn_z_lo_ready")
        z_ig_ready, z_fo_ready = sem("z_ig_ready"), sem("z_fo_ready")
        ig_ready, f_ready, o_ready = sem("ig_ready"), sem("f_ready"), sem("o_ready")
        products_ready = sem("products_ready")
        cell_ready, tanh_cell_ready = sem("cell_ready"), sem("tanh_cell_ready")
        h_scaled_ready, h_hi_ready, h_ready = sem("h_scaled_ready"), sem("h_hi_ready"), sem("h_ready")
        y_ready, y_hi_ready, y_lo_ready = sem("y_ready"), sem("y_hi_ready"), sem("y_lo_ready")
        rnn_z_ready, rnn_tanh_ready = sem("rnn_z_ready"), sem("rnn_tanh_ready")
        rnn_hi_ready, rnn_ready = sem("rnn_hi_ready"), sem("rnn_ready")
        out_summed = sem("out_summed")
        out_turned = sem("out_turned")
        out_copied = sem("out_copied")

        STAGE = {"wx0": stage_wx0, "wh0": stage_wh0, "wx1": stage_wx1, "wh1": stage_wh1}
        PARTS = {"wx0": wx0, "wh0": wh0, "wx1": wx1, "wh1": wh1}
        SOURCE = {"wx0": Wx0, "wh0": Wh0, "wx1": Wx1, "wh1": Wh1}

        def loaded_piece(name, tensor, n):
            return tensor[:, :, GATE_COLUMNS[C * n]:GATE_COLUMNS[C * n] + D] if LOADS[name] == G else tensor[:, :, :]

        def piece(name, tensor, n):
            return loaded_piece(name, tensor, n) if LOADS[name] == G else tensor[:, n, :]

        def scale_name(name, n):
            return name + ("_ig", "_fo")[n // 2] if LOADS[name] == G else name

        def bank(k, m):
            banks = prologue_banks if k.prologue else ps_proj
            return banks[m % len(banks)][:, 0:BT * N]

        def last_bank(s):
            return ps_proj[s % 2][:, 0:C * N].rearrange("p (m n) -> p m n", m=C)

        def both_halves(engine, dram, b):
            pairs = dram.rearrange("n (b r) d -> n b (r d)", r=BT // 2)
            starts = [2 * b + tb if isinstance(b, int) else engine.snap(2 * b + tb) for tb in range(2)]
            return [pairs[:, bass.ds(start, 1), :].rearrange("n o e -> n (o e)") for start in starts]

        block = ctx.enter_context(nc.Block())

        @block.sync
        def _(sp):
            def load_x(parity, halves):
                for tb, rows in enumerate(halves):
                    sp.dma_start(x_rows[parity][tb * N:(tb + 1) * N, :, :].rearrange("p j d -> p (j d)"),
                                 rows).then_inc(x_loaded[parity], 16)

            def load_weights(name):
                rows = SOURCE[name].rearrange("(k p) n -> p k n", p=P)
                for n in range(LOADS[name]):
                    sp.dma_start(loaded_piece(name, STAGE[name], n), loaded_piece(name, rows, n)
                                 ).then_inc(w_loaded[name][n], 16)

            def store_out(halves):
                for tb, rows in enumerate(halves):
                    sp.dma_start(rows, out_rows[tb * N:(tb + 1) * N, :, :].rearrange("p j d -> p (j d)")
                                 ).then_inc(moved, 16)

            load_x(0, both_halves(sp, x, 0))
            load_weights("wx0")
            gates = b0.rearrange("(m p) -> m p", p=P)
            for to, of, count in ((0, 0, C), (C, 3 * C, C), (2 * C, C, 2 * C)):
                sp.dma_start(bias_rows[to:to + count, :], gates[of:of + count, :]).then_inc(moved, 16)
            sp.dma_start(bias_rows[M0:M0 + C, :], b1.rearrange("(m p) -> m p", p=P)).then_inc(moved, 16)
            load_weights("wh0")

            def blocks(k):
                loads = both_halves(sp, x, k.b + 2) if k.load_x else []
                stores = both_halves(sp, out, k.b - 2) if k.out else []
                if k.load_x:
                    if not k.prologue:
                        sp.wait_ge(x_maxed, k.b + 1)
                        sp.wait_ge(x_turned, 2 * k.b + 2)
                    load_x(k.parity, loads)
                if k.prologue:
                    sp.wait_ge(w_lo_ready, PIECES_TO["wx0"])
                    load_weights("wx1")
                    load_weights("wh1")
                if k.out:
                    sp.wait_ge(out_copied, 2 * k.b - 2)
                    store_out(stores)

            run_blocks(sp, blocks)
            for b in (NB - 2, NB - 1):
                sp.wait_ge(out_copied, 2 * b + 2)
                store_out(both_halves(sp, out, b))
            sp.wait_ge(moved, SMALL + 32 * NB)

        @block.gpsimd
        def _(pool):
            nc.gpsimd.memset(ident[:, :], 0.0).then_inc(ident_zeroed, 1)
            pool.wait_ge(ident_zeroed, 1)
            nc.gpsimd.affine_select(out=ident[:, :], in_=ident[:, :], compare_op=ALU.not_equal, fill=1.0,
                                    base=0, pattern=[[-1, P]], channel_multiplier=1).then_inc(ident_ready, 1)

            def max_of_x(b, parity):
                count = b + 1 if isinstance(b, int) else pool.to_reg(b + 1)
                pool.wait_ge(ident_ready, 1)
                pool.wait_ge(x_maxed, count)
                nc.gpsimd.partition_all_reduce(x_max[parity][:, :], x_max_rows[:, :], P,
                                               ABSMAX).then_inc(x_all_maxed, 1)

            def max_over_partitions(name):
                pool.wait_ge(w_part_maxed, NAMES.index(name) + 1)
                nc.gpsimd.partition_all_reduce(all_max[name][:, :], part_max[name][:, :], P,
                                               ABSMAX).then_inc(w_all_maxed, 1)

            max_over_partitions("h0")
            max_of_x(0, 0)
            max_over_partitions("wx0_ig")
            max_over_partitions("wx0_fo")
            max_of_x(1, 1)
            max_over_partitions("wh0_ig")
            max_over_partitions("wh0_fo")

            def blocks(k):
                if k.first:
                    for name in ("wx1", "wh1"):
                        max_over_partitions(name)
                if k.load_x and not k.prologue:
                    max_of_x(k.b + 2, k.parity)

            run_blocks(pool, blocks)

        @block.scalar
        def _(act):
            act.dma_start(h0_rows[:, :], h0).then_inc(h0_loaded, 16)

            def hi_of_weights(name, n):
                act.wait_ge(w_scaled, NAMES.index(scale_name(name, n)) + 1)
                nc.scalar.activation(piece(name, PARTS[name][0], n), piece(name, STAGE[name], n),
                                     ACT.Copy, scale=scale[scale_name(name, n)]).then_inc(w_hi_ready, 1)

            def read_lstm_chunk(k, m):
                if k.prologue and m == IG_CHUNKS[0]:
                    act.wait_ge(x_unscaled, 1)
                if k.prologue and m == FO_CHUNKS[0]:
                    act.wait_ge(x_unscaled, 2)
                act.wait_ge(proj_done, k.lstm_chunk(m) + 1)
                nc.scalar.activation(xz[1 - k.parity][:, m, :], bank(k, m), ACT.Identity,
                                     bias=bias[:, m:m + 1],
                                     scale=unscale_x[1 - k.parity][:, m // (2 * C):m // (2 * C) + 1]).then_inc(proj_read, 1)

            def read_rnn_chunk(k, m):
                act.wait_ge(proj_done, k.rnn_chunk(m) + 1)
                nc.scalar.activation(rxz[:, m, :], ps_proj[m % 2][:, 0:BT * N], ACT.Identity,
                                     bias=bias[:, M0 + m:M0 + m + 1],
                                     scale=unscale_y[:, :]).then_inc(proj_read, 1)

            def read_x(b, parity, j):
                act.wait_ge(x_scaled, b + 1)
                act.wait_ge(x_turned, 2 * b + j + 1)
                nc.scalar.activation(xT[parity][:, j, :, :], ps_turn[:, :, :], ACT.Copy)
                nc.scalar.activation(x_parts[0][:, j, :, :], ps_turn[:, :, :], ACT.Copy,
                                     scale=scale_x[:, :]).then_inc(x_hi_ready, 1)

            def read_last_products(s):
                act.wait_ge(last_proj_done, s + 1)
                act.wait_ge(rnn_z_ready, BT * (NB - 2) + s + 1)
                act.wait_ge(y_unscaled, NB)
                q = place(s)[2]
                for m in range(C):
                    last = nc.scalar.activation(rxz[:, m, q * N:(q + 1) * N], last_bank(s)[:, m, :], ACT.Identity,
                                                bias=bias[:, M0 + m:M0 + m + 1], scale=unscale_y[:, :])
                last.then_inc(last_proj_read, 1)

            def read_out(b, j):
                if j == 0:
                    act.wait_ge(moved, SMALL + 32 * b)
                act.wait_ge(out_turned, 2 * b + j + 1)
                nc.scalar.activation(out_rows[:, j, :], ps_turn[:, :, :].rearrange("p c q -> p (c q)"),
                                     ACT.Copy).then_inc(out_copied, 1)

            def rnn_tanh(r, state_before=True):
                act.wait_ge(rnn_z_ready, r + 1)
                if state_before:
                    act.wait_ge(out_summed, r)
                    act.wait_ge(rnn_ready, r)
                nc.scalar.activation(as_chunks(rnn_h), rnn_z[:, :, :],
                                     ACT.Tanh).then_inc(rnn_tanh_ready, 1)

            def as_chunks(gate):
                return gate[:, :].rearrange("p (c n) -> p c n", c=C)

            act.wait_ge(w_scaled, NAMES.index("h0") + 1)
            for parts in (h_parts, rnn_parts):
                last = nc.scalar.activation(parts[:, :, 0, :], ps_h0, ACT.Copy, scale=scale["h0"])
            last.then_inc(h0_hi_ready, 1)
            read_x(0, 0, 0)
            read_x(0, 0, 1)
            hi_of_weights("wx0", 0)
            hi_of_weights("wx0", 1)
            act.wait_ge(biases_turned, 1)
            nc.scalar.activation(bias[:, :], ps_bias, ACT.Copy).then_inc(biases_read, 1)
            act.wait_ge(biases_read, 1)

            def blocks(k):
                for s in range(BT):
                    t = BT * k.b + s
                    j, tb = s % 2, s // 2
                    if s == 0 and not k.first:
                        chunks = [(read_rnn_chunk, m) for m in range(C)] if k.rnn else []
                    else:
                        chunks = [(read_lstm_chunk, m) for m in k.chunks_in_step[s]] if k.next_x else []

                    def read_chunks(count):
                        for read, m in chunks[:count]:
                            read(k, m)
                        del chunks[:count]

                    if k.rnn_before if s == 0 else k.rnn:
                        rnn_tanh(k.early_rnn_step(s), state_before=k.steady or s >= 2)
                    if k.lstm:
                        act.wait_ge(z_ig_ready, t + 1)
                        nc.scalar.activation(as_chunks(gate_i), z_ig[:, 0:C, :], ACT.Sigmoid)
                        nc.scalar.activation(as_chunks(gate_g), z_ig[:, C:2 * C, :],
                                             ACT.Tanh).then_inc(ig_ready, 1)
                    if s < 2 and k.out:
                        read_out(k.b - 2, s)
                    if s >= 2 and k.last:
                        read_out(k.b - 1, s - 2)
                    if s == 0 and k.rnn:
                        act.wait_ge(y_unscaled, k.b)
                        if k.rnn_before:
                            act.wait_ge(rnn_z_ready, BT * (k.b - 1))
                    if s == (0 if k.first else 1) and k.next_x and not k.prologue:
                        act.wait_ge(x_unscaled, k.b + 3)
                    if k.lstm:
                        read_chunks(1)
                        act.wait_ge(z_fo_ready, t + 1)
                        nc.scalar.activation(as_chunks(gate_f), z_fo[:, 0:C, :], ACT.Sigmoid).then_inc(f_ready, 1)
                        nc.scalar.activation(as_chunks(gate_o), z_fo[:, C:2 * C, :],
                                             ACT.Sigmoid).then_inc(o_ready, 1)
                        read_chunks(1)
                        if s > 0 and k.last:
                            rnn_tanh(k.middle_rnn_step(s))
                        act.wait_ge(cell_ready, t + 1)
                        nc.scalar.activation(tanh_cell[:, :], cell[:, :], ACT.Tanh).then_inc(tanh_cell_ready, 1)
                        read_chunks(2)
                        act.wait_ge(y_ready, t + 1)
                        nc.scalar.activation(
                            y1_parts[k.parity][0][:, :, (2 * j + tb) * N:(2 * j + tb + 1) * N],
                            y1[k.parity][:, 2 * j + tb, :, :], ACT.Copy,
                            scale=scale_y[k.parity][:, :]).then_inc(y_hi_ready, 1)
                    if s > 0 and k.last:
                        read_last_products(s - 1)
                    if k.prologue and s == 1:
                        read_chunks(2)
                        hi_of_weights("wx0", 2)
                        hi_of_weights("wx0", 3)
                    if k.prologue and s == 3:
                        hi_of_weights("wh0", 0)
                        read_chunks(1)
                        hi_of_weights("wh0", 1)
                        read_chunks(len(chunks))
                        hi_of_weights("wh0", 2)
                        read_x(1, 1, 0)
                        hi_of_weights("wh0", 3)
                        read_x(1, 1, 1)
                    if k.first and s in (1, 2):
                        for n in range(C):
                            hi_of_weights(("wx1", "wh1")[s - 1], n)
                            read_chunks(1)
                    read_chunks(len(chunks))
                    if s == 0 and k.next_x and k.rnn:
                        read_x(k.b + 1, 1 - k.parity, 1)
                    if s == BT - 1 and k.load_x and not k.prologue:
                        read_x(k.b + 2, k.parity, 0)

            run_blocks(act, blocks)
            rnn_tanh(T - 2)
            read_last_products(BT - 1)
            read_out(NB - 1, 0)
            rnn_tanh(T - 1)
            read_out(NB - 1, 1)

        @block.vector
        def _(dve):
            own = [0]

            def scale_step(instruction):
                own[0] += 1
                instruction.then_inc(scale_steps, 1)
                dve.wait_ge(scale_steps, own[0])

            def power_below(result, maximum, other=None):
                bits = result.bitcast(U32)
                if other is None:
                    yield nc.vector.tensor_scalar(result, maximum, SMALLEST_MAX, None, ALU.max)
                else:
                    yield nc.vector.scalar_tensor_tensor(result, maximum, SMALLEST_MAX, other, ALU.max, ALU.max)
                yield nc.vector.tensor_scalar(bits, bits, EXPONENT_MASK, None, ALU.bitwise_and)
                yield nc.vector.tensor_scalar(result, result, 1.0 / HIDDEN_SCALE, None, ALU.mult)

            def max_of_piece(name, n):
                dve.wait_ge(w_loaded[name][n if LOADS[name] == G else 0], 16)
                part = scale_name(name, n)
                column = n % MAXIMA[part]
                last = nc.vector.tensor_reduce(part_max[part][:, column:column + 1], piece(name, STAGE[name], n),
                                               AX_XY if LOADS[name] == G else AX_X, ALU.max,
                                               apply_absolute_value=True)
                if column == MAXIMA[part] - 1:
                    last.then_inc(w_part_maxed, 1)

            def scale_of_weights(name):
                dve.wait_ge(w_all_maxed, NAMES.index(name) + 1)
                maxima = [all_max[name][:, i:i + 1] for i in range(MAXIMA[name])]
                if MAXIMA[name] == C:
                    scale_step(nc.vector.tensor_reduce(all_max_whole[:, :], all_max[name][:, :], AX_X, ALU.max))
                    maxima = [all_max_whole[:, :]]
                for step in power_below(inv[name], *maxima):
                    scale_step(step)
                nc.vector.reciprocal(scale[name], inv[name]).then_inc(w_scaled, 1)

            def lo_of_weights(name, n):
                dve.wait_ge(w_hi_ready, PIECES_TO[name] - C + n + 1)
                a, h, l = (piece(name, v, n) for v in (STAGE[name], PARTS[name][0], PARTS[name][1]))
                nc.vector.scalar_tensor_tensor(l, a, scale[scale_name(name, n)], h, ALU.mult,
                                               ALU.subtract).then_inc(w_lo_ready, 1)

            def max_of_x(b, parity, half):
                dve.wait_ge(x_loaded[parity], 32 * half + 32)
                nc.vector.tensor_reduce(x_max_rows[:, :], x_rows[parity][:, :, :].rearrange("p j d -> p (j d)"),
                                        AX_X, ALU.max, apply_absolute_value=True).then_inc(x_maxed, 1)

            def scales_of_block(b, parity):
                dve.wait_ge(x_all_maxed, b + 1)
                nc.vector.tensor_scalar(y_max[:, :], x_max[parity][:, :], 1.0, None, ALU.add
                                        ).then_inc(block_steps, 1)
                count = 7 * b + 1
                for maximum, result in ((x_max[parity], inv_x), (y_max, inv_y[parity])):
                    for step in power_below(result[:, :], maximum[:, :]):
                        step.then_inc(block_steps, 1)
                        count = count + 1
                        dve.wait_ge(block_steps, count)
                nc.vector.reciprocal(scale_x[:, :], inv_x[:, :])
                nc.vector.reciprocal(scale_y[parity][:, :], inv_y[parity][:, :]).then_inc(x_scaled, 1)

            def unscale_of_x(parity):
                nc.vector.tensor_scalar(unscale_x[parity][:, :], inv_wx0, inv_x[:, :], None,
                                        ALU.mult).then_inc(x_unscaled, 1)

            def first_unscale(half):
                nc.vector.tensor_scalar(unscale_x[0][:, half:half + 1], inv_wx0[:, half:half + 1],
                                        inv_x[:, :], None, ALU.mult).then_inc(x_unscaled, 1)

            def lo_of_x(b, parity, j):
                dve.wait_ge(x_hi_ready, 2 * b + j + 1)
                nc.vector.scalar_tensor_tensor(
                    x_parts[1][:, j, :, :].rearrange("p c q -> p (c q)"),
                    xT[parity][:, j, :, :].rearrange("p c q -> p (c q)"), scale_x[:, :],
                    x_parts[0][:, j, :, :].rearrange("p c q -> p (c q)"), ALU.mult,
                    ALU.subtract).then_inc(x_lo_ready, 1)

            def add_products(z, z_lo, products, unscale, inputs, lo_ready, count, ready):
                nc.vector.scalar_tensor_tensor(z_lo[:, :, :], products[:, :, 1, :], unscale, inputs,
                                               ALU.mult, ALU.add).then_inc(lo_ready, 1)
                dve.wait_ge(lo_ready, count)
                nc.vector.scalar_tensor_tensor(z[:, :, :], products[:, :, 0, :], unscale,
                                               z_lo[:, :, :], ALU.mult, ALU.add).then_inc(ready, 1)

            def as_chunks(state):
                return state[:, :].rearrange("p (c n) -> p c n", c=C)

            def second_layer_piece(s, n):
                name = ("wx1", "wh1")[s % 2]
                if s < 2:
                    max_of_piece(name, n)
                else:
                    lo_of_weights(name, n)

            def second_layer_scales(s):
                scale_of_weights(("wx1", "wh1")[s])
                if s == 1:
                    nc.vector.tensor_scalar(rnn_unscale_h[:, :], inv["wh1"], 1.0 / HIDDEN_SCALE, None,
                                            ALU.mult)
                    nc.vector.tensor_tensor(rnn_unscale_first[:, :], inv["wh1"], inv["h0"], ALU.mult)

            def scale_of_y(k):
                nc.vector.tensor_tensor(unscale_y[:, :], inv_y[k.parity][:, :], inv["wx1"],
                                        ALU.mult).then_inc(y_unscaled, 1)

            def lstm_step(k, s):
                t = BT * k.b + s
                j, tb = s % 2, s // 2
                q = 2 * j + tb
                here = slice(q * N, (q + 1) * N)
                unscales = unscale_first if k.first and s == 0 else unscale_h
                dve.wait_ge(ig_done, t + 1)
                add_products(z_ig, z_lo_ig, ps_ig, unscales[:, 0:1], xz[k.parity][:, 0:2 * C, here],
                             z_lo_ready, 2 * t + 1, z_ig_ready)
                if k.first:
                    second_layer_piece(s, 0)
                dve.wait_ge(ig_ready, t + 1)
                nc.vector.tensor_tensor(i_times_g[:, :], gate_i[:, :], gate_g[:, :],
                                        ALU.mult).then_inc(products_ready, 1)
                dve.wait_ge(fo_done, t + 1)
                add_products(z_fo, z_lo_fo, ps_fo, unscales[:, 1:2], xz[k.parity][:, 2 * C:4 * C, here],
                             z_lo_ready, 2 * t + 2, z_fo_ready)
                if k.first:
                    second_layer_piece(s, 1)
                middle = s > 0 and k.last
                if middle:
                    r, step = k.middle_rnn_step(s), 2 * s - 1
                    parity = 1 - k.parity if step < BT else k.parity
                    if step >= BT:
                        dve.wait_ge(last_proj_read, step - BT + 1)
                    rnn_sum(r, step)
                dve.wait_ge(f_ready, t + 1)
                nc.vector.tensor_tensor(f_times_c[:, :], gate_f[:, :], cell[:, :],
                                        ALU.mult).then_inc(products_ready, 1)
                dve.wait_ge(products_ready, 2 * t + 2)
                nc.vector.tensor_tensor(cell[:, :], f_times_c[:, :], i_times_g[:, :],
                                        ALU.add).then_inc(cell_ready, 1)
                if middle:
                    rnn_state(r)
                dve.wait_ge(o_ready, t + 1)
                dve.wait_ge(tanh_cell_ready, t + 1)
                nc.vector.scalar_tensor_tensor(h_scaled[:, :], gate_o[:, :], HIDDEN_SCALE, tanh_cell[:, :],
                                               ALU.mult, ALU.mult).then_inc(h_scaled_ready, 1)
                dve.wait_ge(h_scaled_ready, t + 1)
                nc.vector.tensor_copy(h_parts[:, :, 0, :], as_chunks(h_scaled)).then_inc(h_hi_ready, 1)
                dve.wait_ge(h_hi_ready, t + 1)
                nc.vector.tensor_tensor(h_parts[:, :, 1, :], as_chunks(h_scaled), h_parts[:, :, 0, :],
                                        ALU.subtract).then_inc(h_ready, 1)
                nc.vector.scalar_tensor_tensor(
                    y1[k.parity][:, q, :, :], as_chunks(h_scaled),
                    1.0 / HIDDEN_SCALE, xT[k.parity][:, j, :, tb * N:(tb + 1) * N], ALU.mult,
                    ALU.add).then_inc(y_ready, 1)
                if middle:
                    rnn_out(step, parity)
                dve.wait_ge(y_hi_ready, t + 1)
                nc.vector.scalar_tensor_tensor(
                    y1_parts[k.parity][1][:, :, here], y1[k.parity][:, q, :, :], scale_y[k.parity][:, :],
                    y1_parts[k.parity][0][:, :, here], ALU.mult, ALU.subtract).then_inc(y_lo_ready, 1)

            def rnn_sum(r, s, first=False):
                q = place(s)[2]
                dve.wait_ge(rnn_done, r + 1)
                add_products(rnn_z, rnn_z_lo, ps_rnn, (rnn_unscale_first if first else rnn_unscale_h)[:, :],
                             rxz[:, :, q * N:(q + 1) * N], rnn_z_lo_ready, r + 1, rnn_z_ready)

            def rnn_state(r):
                dve.wait_ge(rnn_tanh_ready, r + 1)
                nc.vector.tensor_scalar(rnn_parts[:, :, 0, :], as_chunks(rnn_h), HIDDEN_SCALE, None,
                                        ALU.mult).then_inc(rnn_hi_ready, 1)
                dve.wait_ge(rnn_hi_ready, r + 1)
                nc.vector.scalar_tensor_tensor(rnn_parts[:, :, 1, :], as_chunks(rnn_h), HIDDEN_SCALE,
                                               rnn_parts[:, :, 0, :], ALU.mult,
                                               ALU.subtract).then_inc(rnn_ready, 1)

            def rnn_out(s, parity):
                j, tb, q = place(s)
                nc.vector.tensor_tensor(outT[:, j, :, tb * N:(tb + 1) * N], y1[parity][:, q, :, :],
                                        as_chunks(rnn_h), ALU.add).then_inc(out_summed, 1)

            def early_rnn_step(k, s):
                r = k.early_rnn_step(s)
                step, parity = (s - 1, 1 - k.parity) if s > 0 else (BT - 1, k.parity)
                if s > 1 and k.last:
                    step = 2 * (s - 1)
                    if step >= BT:
                        step, parity = step - BT, k.parity
                        dve.wait_ge(last_proj_read, step + 1)
                if s == 1:
                    dve.wait_ge(proj_read, k.rnn_chunk(C))
                rnn_sum(r, step, first=k.rnn_first and s == 1)
                rnn_state(r)
                rnn_out(step, parity)

            nc.vector.memset(cell[:, :], 0.0).then_inc(cell_zeroed, 1)
            dve.wait_ge(h0_turned, 1)
            nc.vector.tensor_reduce(part_max["h0"][:, :], ps_h0, AX_XY, ALU.max,
                                    apply_absolute_value=True).then_inc(w_part_maxed, 1)
            max_of_x(0, 0, 0)
            scale_of_weights("h0")
            scales_of_block(0, 0)
            dve.wait_ge(h0_hi_ready, 1)
            for parts in (h_parts, rnn_parts):
                nc.vector.scalar_tensor_tensor(parts[:, :, 1, :], ps_h0, scale["h0"],
                                               parts[:, :, 0, :], ALU.mult,
                                               ALU.subtract).then_inc(h0_lo_ready, 1)
            max_of_piece("wx0", 0)
            max_of_piece("wx0", 1)
            lo_of_x(0, 0, 0)
            lo_of_x(0, 0, 1)
            scale_of_weights("wx0_ig")
            first_unscale(0)
            max_of_piece("wx0", 2)
            lo_of_weights("wx0", 0)
            lo_of_weights("wx0", 1)
            max_of_piece("wx0", 3)
            scale_of_weights("wx0_fo")
            first_unscale(1)
            max_of_piece("wh0", 0)
            lo_of_weights("wx0", 2)
            dve.wait_ge(x_all_maxed, 1)
            max_of_x(1, 1, 0)
            lo_of_weights("wx0", 3)
            max_of_piece("wh0", 1)
            scales_of_block(1, 1)
            unscale_of_x(1)
            scale_of_weights("wh0_ig")
            max_of_piece("wh0", 2)
            max_of_piece("wh0", 3)
            lo_of_weights("wh0", 0)
            scale_of_weights("wh0_fo")
            nc.vector.tensor_scalar(unscale_h[:, :], inv_wh0, 1.0 / HIDDEN_SCALE, None, ALU.mult)
            nc.vector.tensor_scalar(unscale_first[:, :], inv_wh0, inv["h0"], None, ALU.mult)
            for n in (1, 2, 3):
                lo_of_weights("wh0", n)
            lo_of_x(1, 1, 0)
            lo_of_x(1, 1, 1)
            dve.wait_ge(cell_zeroed, 1)

            def blocks(k):
                for s in range(BT):
                    if s < 2 and k.next_x and k.rnn:
                        lo_of_x(k.b + 1, 1 - k.parity, s)
                    if k.rnn_before if s == 0 else k.rnn:
                        early_rnn_step(k, s)
                    if s == 1 and k.last:
                        scale_of_y(k)
                    if k.lstm:
                        lstm_step(k, s)
                    if k.first:
                        second_layer_piece(s, 2)
                        second_layer_piece(s, 3)
                        if s < 2:
                            second_layer_scales(s)
                    if s == 2 and k.load_x and not k.prologue:
                        dve.wait_ge(x_all_maxed, k.b + 2)
                        max_of_x(k.b + 2, k.parity, k.half + 1)
                    if s == BT - 1 and k.lstm and not k.last:
                        scale_of_y(k)
                    if s == BT - 1 and k.load_x and not k.prologue:
                        scales_of_block(k.b + 2, k.parity)
                        unscale_of_x(k.parity)

            run_blocks(dve, blocks)
            for r in (T - 2, T - 1):
                dve.wait_ge(last_proj_read, r - (T - BT) + 1)
                rnn_sum(r, r % BT)
                rnn_state(r)
                rnn_out(r % BT, (NB - 1) % 2)

        @block.tensor
        def _(pe):
            def input_products(result, weights, columns, moving):
                terms = [(k, w, v) for k in range(C) for w, v in ((0, 0), (0, 1), (1, 0))]
                for n, (k, w, v) in enumerate(terms):
                    last = nc.tensor.matmul(result, weights[w][:, k, columns:columns + P], moving(v, k),
                                            start=(n == 0), stop=(n == len(terms) - 1))
                return last

            def recurrent_products(result, weights, columns, parts):
                for k in range(C):
                    hi, lo = (w[:, k, columns:columns + P] for w in weights)
                    both, upper = parts[:, k, :, :].rearrange("p v n -> p (v n)"), parts[:, k, 0, :]
                    whole, first = result.rearrange("p v n -> p (v n)"), result[:, 0, :]
                    if k < C - 1:
                        nc.tensor.matmul(whole, hi, both, start=(k == 0), stop=False)
                        nc.tensor.matmul(first, lo, upper, start=False, stop=False)
                    else:
                        nc.tensor.matmul(first, lo, upper, start=False, stop=False)
                        last = nc.tensor.matmul(whole, hi, both, start=False, stop=True)
                return last

            def turn_x(b, parity, half, j):
                if j == 0:
                    pe.wait_ge(x_loaded[parity], 32 * half + 32)
                for c in range(C):
                    last = nc.tensor.transpose(ps_turn[:, c, :], x_rows[parity][:, j, c * P:(c + 1) * P],
                                               ident[:, :])
                last.then_inc(x_turned, 1)

            def turn_out(b, j):
                pe.wait_ge(out_summed, BT * b + 3 + j)
                for c in range(C):
                    last = nc.tensor.transpose(ps_turn[:, c, :], outT[:, j, c, :], ident[:, :])
                last.then_inc(out_turned, 1)

            def rnn_products(r, first=False):
                if first:
                    pe.wait_ge(h0_lo_ready, 2)
                else:
                    pe.wait_ge(rnn_ready, r)
                for m in range(C):
                    last = recurrent_products(ps_rnn[:, m, :, :], wh1, m * P, rnn_parts)
                last.then_inc(rnn_done, 1)

            def last_products(s):
                pe.wait_ge(y_hi_ready, T - BT + s + 1)
                pe.wait_ge(y_lo_ready, T - BT + s + 1)
                if s >= 2:
                    pe.wait_ge(last_proj_read, s - 1)
                q = place(s)[2]
                for m in range(C):
                    last = input_products(last_bank(s)[:, m, :], wx1, m * P,
                                          lambda v, c: y1_parts[(NB - 1) % 2][v][:, c, q * N:(q + 1) * N])
                last.then_inc(last_proj_done, 1)

            pe.wait_ge(ident_ready, 1)
            pe.wait_ge(h0_loaded, 16)
            for c in range(C):
                last = nc.tensor.transpose(ps_h0[:, c, :], h0_rows[:, c * P:(c + 1) * P], ident[0:N, 0:N])
            last.then_inc(h0_turned, 1)
            turn_x(0, 0, 0, 0)
            pe.wait_ge(x_hi_ready, 1)
            turn_x(0, 0, 0, 1)
            pe.wait_ge(moved, SMALL)
            nc.tensor.transpose(ps_bias, bias_rows[:, :],
                                ident[0:M0 + C, 0:M0 + C]).then_inc(biases_turned, 1)

            def blocks(k):
                for s in range(BT):
                    t = BT * k.b + s
                    if k.lstm:
                        if k.first and s == 0:
                            pe.wait_ge(h0_hi_ready, 1)
                            pe.wait_ge(h0_lo_ready, 2)
                            pe.wait_ge(biases_read, 1)
                        else:
                            pe.wait_ge(h_ready, t)
                        if s == 0:
                            pe.wait_ge(proj_read, k.evacuated_before())
                        for half, (result, chunks, done) in enumerate(((ps_ig, IG_CHUNKS, ig_done),
                                                                       (ps_fo, FO_CHUNKS, fo_done))):
                            if k.first and s == 0 and half == 1:
                                pe.wait_ge(x_hi_ready, 3)
                                turn_x(1, 1, 0, 1)
                            if k.first and s == 0:
                                pe.wait_ge(w_lo_ready, PIECES_TO["wx0"] + 2 * half + 2)
                            for m in chunks:
                                last = recurrent_products(result[:, m - chunks[0], :, :], wh0,
                                                          GATE_COLUMNS[m], h_parts)
                            last.then_inc(done, 1)
                    if s == 0 and k.out:
                        if k.next_x:
                            pe.wait_ge(x_hi_ready, 2 * k.b + 3)
                        else:
                            pe.wait_ge(out_copied, 2 * k.b - 4)
                        turn_out(k.b - 2, 0)
                    if s == 0 and k.rnn:
                        if k.rnn_first:
                            pe.wait_ge(w_lo_ready, PIECES_TO["wh1"])
                        pe.wait_ge(y_hi_ready, BT * k.b)
                        pe.wait_ge(y_lo_ready, BT * k.b)
                        for m in range(C):
                            pe.wait_ge(proj_read, k.rnn_chunk(m) - 1)
                            input_products(ps_proj[m % 2][:, 0:BT * N], wx1, m * P,
                                           lambda v, c: y1_parts[1 - k.parity][v][:, c, :]
                                           ).then_inc(proj_done, 1)
                    if s == 0 and k.next_x and k.rnn:
                        if k.out:
                            pe.wait_ge(out_copied, 2 * k.b - 3)
                        else:
                            pe.wait_ge(x_hi_ready, 2 * k.b + 3)
                        turn_x(k.b + 1, 1 - k.parity, k.half + k.parity, 1)
                    if s == 1 and k.out:
                        if k.next_x:
                            pe.wait_ge(x_hi_ready, 2 * k.b + 4)
                        else:
                            pe.wait_ge(out_copied, 2 * k.b - 3)
                        turn_out(k.b - 2, 1)
                    if s >= 2 and k.last:
                        pe.wait_ge(out_copied, 2 * (k.b - 1) + s - 2)
                        turn_out(k.b - 1, s - 2)
                    if s > 0 and k.last:
                        rnn_products(k.middle_rnn_step(s))
                        if s == 1:
                            pe.wait_ge(proj_read, k.rnn_chunk(C))
                        last_products(s - 1)
                    if (s > 0 or k.first) and k.next_x:
                        if s == (0 if k.first else 1):
                            pe.wait_ge(x_lo_ready, 2 * (k.b + 1) + 2)
                        for m in k.chunks_in_step[s]:
                            if k.prologue and m % C == 0:
                                pe.wait_ge(w_lo_ready, m // C + 1)
                            if not k.prologue:
                                pe.wait_ge(proj_read, k.lstm_chunk(m) - 1)
                            elif m >= len(prologue_banks):
                                pe.wait_ge(proj_read, m - len(prologue_banks) + 1)
                            input_products(bank(k, m), wx0, GATE_COLUMNS[m],
                                           lambda v, c: x_parts[v][:, :, c, :]).then_inc(proj_done, 1)
                    if s == BT - 1 and k.load_x:
                        if k.out:
                            pe.wait_ge(out_copied, 2 * k.b - 2)
                        else:
                            pe.wait_ge(x_hi_ready, 2 * k.b + 4)
                        turn_x(k.b + 2, k.parity, k.half + 1, 0)
                    if k.rnn:
                        rnn_products(k.late_rnn_step(s), first=k.rnn_first and s == 0)

            run_blocks(pe, blocks)
            last_products(BT - 1)
            rnn_products(T - 1)
            for j in range(J):
                pe.wait_ge(out_copied, 2 * (NB - 1) + j)
                turn_out(NB - 1, j)


def kernel(x, cond_1024, L0_cond_Wx, L0_cond_Wh, L0_cond_b, L1_cond_Wx, L1_cond_Wh, L1_cond_b):
    import numpy as np
    import concourse.bacc as bacc
    from concourse.bass_utils import run_bass_kernel_spmd

    nc = bacc.Bacc("TRN2", target_bir_lowering=False, num_devices=1)
    given = {"x": x, "h0": cond_1024, "Wx0": L0_cond_Wx, "Wh0": L0_cond_Wh, "b0": L0_cond_b,
             "Wx1": L1_cond_Wx, "Wh1": L1_cond_Wh, "b1": L1_cond_b}
    arrays = {f"in_{name}": np.ascontiguousarray(a) for name, a in given.items()}
    aps = [nc.dram_tensor(name, a.shape, F32, kind="ExternalInput").ap() for name, a in arrays.items()]
    out = nc.dram_tensor("out", (N, T, D), F32, kind="ExternalOutput").ap()
    build(nc, *aps, out)
    result = run_bass_kernel_spmd(nc, [arrays], core_ids=[0])
    return result.results[0]["out"]
```
